# Optimizing a Trainium2 kernel written in Bass

```python
import numpy as np
import jax
import jax.numpy as jnp

def _softmax(x, axis=-1):
    return jax.nn.softmax(x, axis=axis)

def _gelu(x):
    return jax.nn.gelu(x, approximate=True)

def _silu(x):
    return jax.nn.silu(x)

def _sigmoid(x):
    return jax.nn.sigmoid(x)

def _layernorm(x, axis=-1, eps=1e-05):
    m = jnp.mean(x, axis=axis, keepdims=True)
    v = jnp.var(x, axis=axis, keepdims=True)
    return (x - m) / jnp.sqrt(v + eps)

def _scatter_add(tgt, idx, src, axis=0):
    return tgt.at[idx].add(src)

def _segment_sum(src, seg, n):
    return jax.ops.segment_sum(src, seg, n)
kernel_name = 'mk_metaformer_d1_conv_nhwc512_r4_4f874f'

def setup_inputs(seed: int=0):
    np.random.seed(seed)
    _w = jnp.asarray

    def _rec_inputs():
        import jax
        import jax.numpy as jnp
        _gk = jax.random.key(seed)
        x = -0.0003929 + 0.9999 * jax.random.normal(jax.random.fold_in(_gk, 1), (8, 16, 16, 128), jnp.float32)
        return x
    x = _rec_inputs()

    def _L0_conv_setup():
        import jax, jax.numpy as jnp
        import numpy as np
        HEADS = 8
        DIM_HEAD = 16
        LN_EPS = 1e-05

        def _layernorm(x, gamma, beta):
            mu = jnp.mean(x, axis=-1, keepdims=True)
            var = jnp.mean(jnp.square(x - mu), axis=-1, keepdims=True)
            return (x - mu) * jax.lax.rsqrt(var + LN_EPS) * gamma + beta
        key = jax.random.key(seed)
        k1, k2 = jax.random.split(key)
        B, L, W, C = (8, 16, 16, 128)
        inner = HEADS * DIM_HEAD
        x = jax.random.normal(k1, (B, L, W, C), dtype=jnp.float32)
        w_qkv = jax.random.normal(k2, (C, 3 * inner), dtype=jnp.float32) * 0.02
        q_gamma = jnp.ones((DIM_HEAD,), dtype=jnp.float32)
        q_beta = jnp.zeros((DIM_HEAD,), dtype=jnp.float32)
        k_gamma = jnp.ones((DIM_HEAD,), dtype=jnp.float32)
        k_beta = jnp.zeros((DIM_HEAD,), dtype=jnp.float32)
        return {'x': x, 'w_qkv': w_qkv, 'q_gamma': q_gamma, 'q_beta': q_beta, 'k_gamma': k_gamma, 'k_beta': k_beta}
    _L0_conv_all = _L0_conv_setup()
    _L0_conv_in = {k: v for k, v in _L0_conv_all.items() if k in ('w_qkv', 'q_gamma', 'q_beta', 'k_gamma', 'k_beta')}
    del _L0_conv_all

    def _L0_ffn_setup():
        import jax, jax.numpy as jnp
        import numpy as np
        DIM = 128
        NE = 8
        TOPK = 2
        CF = 1.2
        HID = 4 * DIM
        B, S = (8, 1024)
        key = jax.random.key(seed)
        ks = jax.random.split(key, 4)
        s = 0.02
        return {'x': jax.random.normal(ks[0], (B, S, DIM), jnp.float32), 'gate_w': jax.random.normal(ks[1], (NE, DIM), jnp.float32) * s, 'gate_b': jnp.zeros((NE,), jnp.float32), 'w1': jax.random.normal(ks[2], (NE, DIM, HID), jnp.float32) * s, 'b1': jnp.zeros((NE, HID), jnp.float32), 'w2': jax.random.normal(ks[3], (NE, HID, DIM), jnp.float32) * s, 'b2': jnp.zeros((NE, DIM), jnp.float32)}
    _L0_ffn_all = _L0_ffn_setup()
    _L0_ffn_in = {k: v for k, v in _L0_ffn_all.items() if k in ('gate_w', 'gate_b', 'w1', 'b1', 'w2', 'b2')}
    del _L0_ffn_all
    return {'x': x, 'L0_conv_w_qkv': _L0_conv_in['w_qkv'], 'L0_conv_q_gamma': _L0_conv_in['q_gamma'], 'L0_conv_q_beta': _L0_conv_in['q_beta'], 'L0_conv_k_gamma': _L0_conv_in['k_gamma'], 'L0_conv_k_beta': _L0_conv_in['k_beta'], 'L0_ffn_gate_w': _L0_ffn_in['gate_w'], 'L0_ffn_gate_b': _L0_ffn_in['gate_b'], 'L0_ffn_w1': _L0_ffn_in['w1'], 'L0_ffn_b1': _L0_ffn_in['b1'], 'L0_ffn_w2': _L0_ffn_in['w2'], 'L0_ffn_b2': _L0_ffn_in['b2']}

def reference(x, L0_conv_w_qkv, L0_conv_q_gamma, L0_conv_q_beta, L0_conv_k_gamma, L0_conv_k_beta, L0_ffn_gate_w, L0_ffn_gate_b, L0_ffn_w1, L0_ffn_b1, L0_ffn_w2, L0_ffn_b2):
    import jax
    import jax.numpy as jnp

    def _L0_conv_ref(x, w_qkv, q_gamma, q_beta, k_gamma, k_beta):
        import jax, jax.numpy as jnp
        import numpy as np
        HEADS = 8
        DIM_HEAD = 16
        LN_EPS = 1e-05

        def _layernorm(x, gamma, beta):
            mu = jnp.mean(x, axis=-1, keepdims=True)
            var = jnp.mean(jnp.square(x - mu), axis=-1, keepdims=True)
            return (x - mu) * jax.lax.rsqrt(var + LN_EPS) * gamma + beta
        B, L, W, C = x.shape
        n = L * W
        xf = x.reshape(B, n, C)
        qkv = xf @ w_qkv
        q, k, v = jnp.split(qkv, 3, axis=-1)

        def to_heads(t):
            return t.reshape(B, n, HEADS, DIM_HEAD).transpose(0, 2, 1, 3)
        q, k, v = (to_heads(q), to_heads(k), to_heads(v))
        q = _layernorm(q, q_gamma, q_beta)
        k = _layernorm(k, k_gamma, k_beta)
        dots = jnp.einsum('bhnd,bhne->bhde', k, v)
        out = jnp.einsum('bhnd,bhde->bhne', q, dots) * (1.0 / n)
        out = out.transpose(0, 2, 1, 3).reshape(B, L, W, HEADS * DIM_HEAD)
        return out

    def _L0_ffn_ref(x, gate_w, gate_b, w1, b1, w2, b2):
        import jax, jax.numpy as jnp
        import numpy as np
        DIM = 128
        NE = 8
        TOPK = 2
        CF = 1.2
        HID = 4 * DIM
        B, S = (8, 1024)
        Bq, Sq, D = x.shape
        T = Bq * Sq
        cap = int(CF * T / NE)
        xf = x.reshape(T, D)
        probs = jax.nn.softmax(xf @ gate_w.T + gate_b, axis=-1)
        topw, topi = jax.lax.top_k(probs, TOPK)
        onehot = jax.nn.one_hot(topi, NE, dtype=topw.dtype)
        w_te = jnp.einsum('tk,tke->te', topw, onehot)
        routed = onehot.sum(axis=1) > 0
        wm = jnp.where(routed, w_te, -1.0)
        sel_w, sel_idx = jax.lax.top_k(wm.T, cap)
        sel_w = jnp.maximum(sel_w, 0.0)
        xg = xf[sel_idx]
        h = jax.nn.gelu(jnp.einsum('ecd,edh->ech', xg, w1) + b1[:, None, :], approximate=False)
        out = jnp.einsum('ech,ehd->ecd', h, w2) + b2[:, None, :]
        weighted = out * sel_w[..., None]
        of = jnp.zeros((T, D), x.dtype).at[sel_idx.reshape(-1)].add(weighted.reshape(-1, D))
        return of.reshape(Bq, Sq, D)

    def _gn(v, G=32, eps=1e-05):
        B_, H_, W_, C_ = v.shape
        g = v.reshape(B_, H_, W_, G, C_ // G)
        m = jnp.mean(g, axis=(1, 2, 4), keepdims=True)
        s = jnp.var(g, axis=(1, 2, 4), keepdims=True)
        return ((g - m) / jnp.sqrt(s + eps)).reshape(v.shape)

    def _ln_c(v, eps=1e-06):
        m = jnp.mean(v, axis=-1, keepdims=True)
        s = jnp.var(v, axis=-1, keepdims=True)
        return (v - m) / jnp.sqrt(s + eps)

    def _ln_t(v, eps=1e-05):
        m = jnp.mean(v, axis=-1, keepdims=True)
        s = jnp.var(v, axis=-1, keepdims=True)
        return (v - m) / jnp.sqrt(s + eps)

    def _to_tokens(v):
        B_, H_, W_, C_ = v.shape
        return v.reshape(B_, H_ * W_, C_)

    def _from_tokens(t, like):
        return t.reshape(like.shape)
    x = x + _L0_conv_ref(_ln_c(x), L0_conv_w_qkv, L0_conv_q_gamma, L0_conv_q_beta, L0_conv_k_gamma, L0_conv_k_beta)
    t = _to_tokens(x)
    t = t + _L0_ffn_ref(_ln_t(t), L0_ffn_gate_w, L0_ffn_gate_b, L0_ffn_w1, L0_ffn_b1, L0_ffn_w2, L0_ffn_b2)
    x = _from_tokens(t, x)
    return x

_drawn_inputs = setup_inputs


def setup_inputs(seed=0):
    import zlib

    import numpy as np

    out = dict(_drawn_inputs(seed))
    spreads = {'L0_conv_q_gamma': (1.0, 0.534),
     'L0_conv_q_beta': (0.0, 0.704),
     'L0_conv_k_gamma': (1.0, 0.2),
     'L0_conv_k_beta': (0.0, 0.8),
     'L0_ffn_gate_b': (0.0, 0.8),
     'L0_ffn_b1': (0.0, 0.8),
     'L0_ffn_b2': (0.0, 0.434)}
    factors = {'L0_ffn_gate_w': 2.836, 'L0_ffn_w1': 5.593, 'L0_ffn_w2': 5.106}
    for name, (base, spread) in spreads.items():
        noise = np.random.default_rng([zlib.crc32(name.encode()), seed]).standard_normal(out[name].shape)
        drawn = base * np.exp(spread * noise) if base else spread * noise
        out[name] = jnp.asarray(drawn.astype(out[name].dtype))
    for name, factor in factors.items():
        out[name] = (out[name] * factor).astype(out[name].dtype)
    return out
```

```python
from contextlib import ExitStack

import numpy as np

import concourse.bass as bass
from concourse import mybir

F32 = mybir.dt.float32
F16 = mybir.dt.float16
BF16 = mybir.dt.bfloat16
I32 = mybir.dt.int32
U32 = mybir.dt.uint32
ALU = mybir.AluOpType
ACT = mybir.ActivationFunctionType
AX = mybir.AxisListType.X

P = 128
HEADS, DH = 8, 16
GROUP = 4
TOPK = 2
CAP_FACTOR = 1.2
LN_C_EPS, LN_H_EPS, LN_T_EPS = 1e-6, 1e-5, 1e-5
DIGIT = 3
BITS = 30


def build(nc, x, w_qkv, q_gamma, q_beta, k_gamma, k_beta, gate_w, gate_b, w1, b1, w2, b2, out):
    B, L, W, C = x.shape
    N = L * W
    T = B * N
    E, _, HID = w1.shape
    NT = T // P
    TPB = N // P
    NG = NT // GROUP
    BPG = GROUP // TPB
    HC = HID // P
    CAP = int(CAP_FACTOR * T / E)
    CHUNKS = [(c * P, min(P, CAP - c * P)) for c in range(-(-CAP // P))]
    NC = len(CHUNKS)
    TE = NT * E
    ROW = C + E
    SUB = 8
    MAJ = P // SUB
    CM = NC * SUB
    CAND = 2 ** DIGIT - 1
    ROUNDS = BITS // DIGIT
    assert C == P and TE == P and HEADS * DH == C and GROUP % TPB == 0

    x_d = x.rearrange("b l w c -> (b l w) c").rearrange("(t p) c -> p t c", p=P)
    out_rows = out.rearrange("b l w c -> (b l w) c")
    out_d = out_rows.rearrange("(t p) c -> p t c", p=P)
    table = nc.dram_tensor("table", [T, ROW], F32, kind="Internal").ap()
    table_d = table.rearrange("(t p) c -> p t c", p=P)

    with ExitStack() as ctx:
        def sb(name, shape, dt=F32):
            return ctx.enter_context(nc.sbuf_tensor(name, shape, dt))

        def sem(name):
            return ctx.enter_context(nc.semaphore(name))

        x_sb = sb("x_sb", [P, NT, C])
        wqkv = sb("wqkv", [C, 3 * C])
        vecs = sb("vecs", [P, 4, DH])
        gate_rows = sb("gate_rows", [E, C])
        gate_bias = sb("gate_bias", [P, E])
        b1_rows = sb("b1_rows", [E * HC, P])
        b2_sb = sb("b2_sb", [P, E, C])
        w1_sb = sb("w1_sb", [C, E, HID])
        w2_sb = sb("w2_sb", [P, E, HC, C])
        ident = sb("ident", [P, P])
        ones = sb("ones", [P, P])
        head_mask = sb("head_mask", [P, P])
        head_mean = sb("head_mean", [P, P])
        diff = sb("diff", [P, P], I32)
        same_e = sb("same_e", [P, P], BF16)
        before_e = sb("before_e", [P, P], BF16)
        token_id = sb("token_id", [P, NT])
        iota_maj = sb("iota_maj", [P, MAJ])
        iota_cm = sb("iota_cm", [P, CM])
        digits = sb("digits", [P, CAND], I32)
        expert_run = sb("expert_run", [P, TE])
        spread = sb("spread", [MAJ, SUB, P], F16)
        eps = sb("eps", [P, 2])
        w_c = sb("w_c", [C, 3 * C])
        w_sum = sb("w_sum", [C, 2 * HEADS])
        vec_rows = sb("vec_rows", [P, 4, HEADS, DH])
        gamma_col = sb("gamma_col", [P, 2])
        qbeta_mat = sb("qbeta_mat", [P, P])
        stat = sb("stat", [P, NT, 6])
        mv = sb("mv", [P, NT, 2])
        std = sb("std", [P, NT])
        rstd = sb("rstd", [P, NT])
        xn = sb("xn", [P, NT, C])
        xnT = sb("xnT", [C, T])
        q_work = sb("q_work", [P, 2, T])
        qT, qsqT = q_work[:, 0, :], q_work[:, 1, :]
        kv = sb("kv", [P, NT, 2 * C])
        ksq = sb("ksq", [P, NT, C])
        kss = sb("kss", [P, NT, HEADS])
        std_qk = sb("std_qk", [P, NT, 2 * HEADS])
        r_qk = sb("r_qk", [P, NT, 2 * HEADS])
        kn = ksq
        beta_v = sb("beta_v", [P, B, P])
        dots = sb("dots", [P, B, P])
        dots_b = sb("dots_b", [P, B, P])
        dots_q = sb("dots_q", [P, B, P])
        att = sb("att", [P, NT, C])
        xb = sb("xb", [P, NT, C])
        x1 = att
        stat2 = sb("stat2", [P, NT, 6])
        mv2 = sb("mv2", [P, NT, 2])
        std2 = sb("std2", [P, NT])
        rstd2 = sb("rstd2", [P, NT])
        rows = sb("rows", [P, NT, ROW])
        x2T = xnT
        gateT = sb("gateT", [C, E])
        b1T = sb("b1T", [P, E * HC])
        logit = sb("logit", [P, NT, E])
        shifted = sb("shifted", [P, NT, E])
        expd = sb("expd", [P, NT, E])
        prob = sb("prob", [P, NT, E])
        g1 = sb("g1", [P, NT, E])
        g2 = sb("g2", [P, NT, E])
        g3 = sb("g3", [P, NT, E])
        g4 = sb("g4", [P, NT, E])
        s1 = sb("s1", [P, NT])
        s2 = sb("s2", [P, NT])
        s3 = sb("s3", [P, NT])
        s4 = sb("s4", [P, NT])
        s5 = sb("s5", [P, NT])
        wT = sb("wT", [TE, P])
        cand = sb("cand", [TE, 2, CAND], I32)
        hits = sb("hits", [TE, CAND, P], BF16)
        count = sb("count", [TE, 2, CAND], BF16)
        best = sb("best", [TE, 2, CAND + 1])
        above = sb("above", [TE, P])
        level = sb("level", [TE, P])
        cnt2 = sb("cnt2", [TE, 2], BF16)
        tot = sb("tot", [TE, 4])
        need = sb("need", [TE, 1])
        run_above = sb("run_above", [TE, P])
        run_level = sb("run_level", [TE, P])
        zeros = sb("zeros", [TE, P])
        ones_te = ones
        taken = sb("taken", [TE, P])
        pos = sb("pos", [TE, P])
        slot_f = sb("slot_f", [P, TE])
        slot = sb("slot", [P, TE], I32)
        maj = sb("maj", [P, TE], I32)
        mnr = sb("mnr", [P, TE], I32)
        chk = sb("chk", [P, TE], I32)
        cm = sb("cm", [P, TE], I32)
        oh_maj = sb("oh_maj", [P, E, NT, MAJ], F16)
        oh_tok = sb("oh_tok", [P, E, NT, MAJ], F16)
        oh_cm = sb("oh_cm", [P, E, NT, CM], F16)
        grid = sb("grid", [MAJ, E, CM], F16)
        index = sb("index", [P, E, NC], U32)
        xg = kv[:, :, :].rearrange("p t c -> p (t c)")[:, 0:E * NC * ROW].rearrange(
            "p (e n r) -> p e n r", e=E, n=NC)
        xgT = sb("xgT", [C, 2, CAP])
        hid = sb("hid", [P, 2, HC, CAP])
        yb = sb("yb", [P, 2, NC, C])
        y = q_work[:, :, :].rearrange("p a t -> p (a t)")[:, 0:E * NC * C].rearrange(
            "p (e n c) -> p e n c", e=E, n=NC)

        banks = [ctx.enter_context(nc.psum_tensor(f"bank{i}", [P, 512], F32)) for i in range(8)]
        ps_T = [banks[0], banks[1]]
        ps_q = banks[2]
        ps_kv = [banks[3], banks[4]]
        ps_d = banks[5]
        ps_o = banks[6]
        misc = banks[7]
        ps_qss = misc[:, 0:128]
        ps_logit = misc[:, 128:256]
        ps_small = misc[:, 256:512]
        ps_h = [banks[2], banks[3], banks[4], banks[5]]
        ps_x = banks[0]
        ps_y = banks[1]
        ps_grid = banks[6]
        ps_cnt = banks[7]

        x_in = [sem(f"x_in{g}") for g in range(NG)]
        wqkv_in, vecs_in, gate_in, b_in, w1_in, w2_in = (sem(n) for n in (
            "wqkv_in", "vecs_in", "gate_in", "b_in", "w1_in", "w2_in"))
        pool_step, dve_step = sem("pool_step"), sem("dve_step")
        const_ready, diff_ready, same_ready, before_ready = (
            sem("const_ready"), sem("diff_ready"), sem("same_ready"), sem("before_ready"))
        wsum_done, wc_ready, vec_ready = sem("wsum_done"), sem("wc_ready"), sem("vec_ready")
        small_T, small_ready, small_act = sem("small_T"), sem("small_ready"), sem("small_act")
        var_ready, std_ready, xn_ready = sem("var_ready"), sem("std_ready"), sem("xn_ready")
        T_done, T_copied = sem("T_done"), sem("T_copied")
        q_done, q_copied, kv_done, kv_copied = sem("q_done"), sem("q_copied"), sem("kv_done"), sem("kv_copied")
        qss_done, kss_ready, stdqk_ready, rqk_ready, kn_ready = (
            sem("qss_done"), sem("kss_ready"), sem("stdqk_ready"), sem("rqk_ready"), sem("kn_ready"))
        d_done, betav_ready, dots_ready, dotsq_ready, o_done, o_used, x1_ready = (
            sem("d_done"), sem("betav_ready"), sem("dots_ready"), sem("dotsq_ready"), sem("o_done"), sem("o_used"), sem("x1_ready"))
        var2_ready, std2_ready, x2_ready = sem("var2_ready"), sem("std2_ready"), sem("x2_ready")
        T2_done, T2_copied, logit_done = sem("T2_done"), sem("T2_copied"), sem("logit_done")
        shifted_ready, exp_ready, routed_ready, wT_done = (
            sem("shifted_ready"), sem("exp_ready"), sem("routed_ready"), sem("wT_done"))
        counted, summed = sem("counted"), sem("summed")
        pos_ready, slotT_done = sem("pos_ready"), sem("slotT_done")
        onehot_ready, grid_done, grid_ready, index_done, index_ready = (
            sem("onehot_ready"), sem("grid_done"), sem("grid_ready"), sem("index_done"), sem("index_ready"))
        gathered = [sem(f"gathered{e}") for e in range(E)]
        xgT_done, xgT_ready, h_done, h_ready, y_done, y_ready = (
            sem("xgT_done"), sem("xgT_ready"), sem("h_done"), sem("h_ready"), sem("y_done"), sem("y_ready"))
        table_out, out_init = sem("table_out"), sem("out_init")
        added = [sem(f"added{e}") for e in range(E)]

        block = ctx.enter_context(nc.Block())

        def tiles(g):
            return slice(g * GROUP, (g + 1) * GROUP)

        def img(b):
            return slice(b * TPB, (b + 1) * TPB)

        def wide(g):
            return slice(g * GROUP * P, (g + 1) * GROUP * P)

        @block.sync
        def _(sp):
            for g in range(NG):
                sp.dma_start(x_sb[:, tiles(g), :], x_d[:, tiles(g), :]).then_inc(x_in[g], 16)
                if g == 0:
                    sp.dma_start(wqkv[:, :], w_qkv).then_inc(wqkv_in, 16)
            sp.dma_start(w1_sb[:, :, :], w1.rearrange("e c h -> c e h")).then_inc(w1_in, 16)
            sp.dma_start(w2_sb[:, :, :, :].rearrange("p e c d -> p (e c) d"),
                         w2.rearrange("e (c p) d -> p (e c) d", p=P)).then_inc(w2_in, 16)
            for g in range(NG):
                sp.wait_ge(x1_ready, BPG * (g + 1))
                sp.dma_start(out_d[:, tiles(g), :], x1[:, tiles(g), :]).then_inc(out_init, 16)
            sp.wait_ge(x2_ready, NT)
            sp.wait_ge(routed_ready, 1)
            sp.dma_start(table_d, rows[:, :, :]).then_inc(table_out, 16)
            sp.wait_ge(out_init, 16 * NG)
            sp.wait_ge(table_out, 16)
            for e in range(E):
                sp.wait_ge(added[e], 16 * NC)

        @block.gpsimd
        def _(pool):
            steps = [0]

            def link(ins):
                steps[0] += 1
                ins.then_inc(pool_step, 1)
                pool.wait_ge(pool_step, steps[0])

            pool.memset(ident[:, :], 0.0)
            pool.memset(ones[:, :], 1.0)
            pool.memset(eps[:, 0:1], LN_C_EPS)
            pool.memset(eps[:, 1:2], LN_H_EPS)
            pool.memset(zeros[:, :], 0.0)
            pool.memset(expert_run[:, :], 1.0)
            pool.iota(digits[:, :], [[1, CAND]], base=1, channel_multiplier=0)
            pool.iota(diff[:, :], [[-1, P]], base=P, channel_multiplier=1)
            pool.iota(token_id[:, :], [[P, NT]], base=0, channel_multiplier=1, allow_small_or_imprecise_dtypes=True)
            pool.iota(iota_maj[:, :], [[1, MAJ]], base=0, channel_multiplier=0, allow_small_or_imprecise_dtypes=True)
            pool.iota(iota_cm[:, :], [[1, CM]], base=0, channel_multiplier=0, allow_small_or_imprecise_dtypes=True)
            link(pool.memset(spread[:, :, :], 0.0))
            pool.memset(expert_run[:, :].rearrange("p (t e) -> p t e", e=E)[:, :, 0:1], 0.0)
            pool.affine_select(out=ident[:, :], in_=ident[:, :], compare_op=ALU.not_equal, fill=1.0,
                               base=0, pattern=[[-1, P]], channel_multiplier=1)
            pool.affine_select(out=spread[:, :, :], in_=spread[:, :, :], compare_op=ALU.not_equal, fill=1.0,
                               base=0, pattern=[[-1, SUB], [1, P]], channel_multiplier=-SUB)
            hm = head_mask[:, :].rearrange("p (h d) -> p h d", d=DH)
            link(pool.affine_select(out=hm, in_=ones[:, :].rearrange("p (h d) -> p h d", d=DH),
                                    compare_op=ALU.is_ge, fill=0.0, base=0,
                                    pattern=[[-DH, HEADS], [0, DH]], channel_multiplier=1))
            link(pool.affine_select(out=hm, in_=hm, compare_op=ALU.is_ge, fill=0.0, base=DH - 1,
                                    pattern=[[DH, HEADS], [0, DH]], channel_multiplier=-1))
            pool.tensor_scalar(head_mean[:, :], head_mask[:, :], 1.0 / N, None, ALU.mult).then_inc(const_ready, 1)
            pool.wait_ge(same_ready, 1)
            pool.affine_select(out=before_e[:, :], in_=same_e[:, :], compare_op=ALU.is_gt, fill=0.0,
                               base=0, pattern=[[1, P]], channel_multiplier=-1).then_inc(before_ready, 1)

            def scale_k(b):
                pool.wait_ge(kv_copied, 2 * (b + 1))
                pool.wait_ge(rqk_ready, b // BPG + 1)
                pool.tensor_tensor(kn[:, img(b), :].rearrange("p t (h d) -> p t h d", d=DH),
                                   kv[:, img(b), 0:C].rearrange("p t (h d) -> p t h d", d=DH),
                                   r_qk[:, img(b), HEADS:2 * HEADS].unsqueeze(3).broadcast_to([P, TPB, HEADS, DH]),
                                   ALU.mult).then_inc(kn_ready, 1)

            def residual(b):
                pool.wait_ge(o_used, b + 1)
                pool.tensor_tensor(x1[:, img(b), :], att[:, img(b), :], xb[:, img(b), :], ALU.add).then_inc(x1_ready, 1)

            for step in range(NG + 2):
                g = step - 1
                if 0 <= g < NG:
                    for b in range(g * BPG, (g + 1) * BPG):
                        scale_k(b)
                    for b in range(g * BPG, (g + 1) * BPG):
                        residual(b)

            def gather(e):
                pool.wait_ge(index_ready, e + 1)
                if e == 0:
                    pool.wait_ge(table_out, 16)
                for c, (_, n) in enumerate(CHUNKS):
                    pool.indirect_dma_start(
                        out=xg[0:n, e, c, :], out_offset=None, in_=table,
                        in_offset=bass.IndirectOffsetOnAxis(ap=index[0:n, e, c:c + 1], axis=0)).then_inc(gathered[e], 16)

            def scatter(e):
                if e == 0:
                    pool.wait_ge(out_init, 16 * NG)
                else:
                    pool.wait_ge(added[e - 1], 16 * NC)
                pool.wait_ge(y_ready, e + 1)
                for c, (_, n) in enumerate(CHUNKS):
                    pool.indirect_dma_start(
                        out=out_rows, out_offset=bass.IndirectOffsetOnAxis(ap=index[0:n, e, c:c + 1], axis=0),
                        in_=y[0:n, e, c, :], in_offset=None, compute_op=ALU.add).then_inc(added[e], 16)

            gather(0)
            gather(1)
            for e in range(E):
                if e + 2 < E:
                    gather(e + 2)
                scatter(e)

        @block.scalar
        def _(act):
            for k, v in enumerate((q_gamma, q_beta, k_gamma, k_beta)):
                act.dma_start(vecs[:, k, :], v.partition_broadcast(P)).then_inc(vecs_in, 16)
            act.dma_start(gate_rows[:, :], gate_w).then_inc(gate_in, 16)
            act.dma_start(gate_bias[:, :], gate_b.partition_broadcast(P)).then_inc(gate_in, 16)
            act.dma_start(b1_rows[:, :], b1.rearrange("e (c p) -> (e c) p", p=P)).then_inc(b_in, 16)
            act.dma_start(b2_sb[:, :, :].rearrange("p e c -> p (e c)"),
                          b2.rearrange("e c -> (e c)").partition_broadcast(P)).then_inc(b_in, 16)
            act.wait_ge(const_ready, 1)

            def norm(g):
                act.wait_ge(var_ready, g + 1)
                act.activation(std[:, tiles(g)], mv[:, tiles(g), 1], ACT.Sqrt, bias=eps[:, 0:1]).then_inc(std_ready, 1)
                act.wait_ge(T_done, g + 1)
                act.activation(xnT[:, wide(g)], ps_T[g % 2][:, :], ACT.Copy).then_inc(T_copied, 1)

            def project(g):
                act.wait_ge(q_done, g + 1)
                act.activation(qT[:, wide(g)], ps_q[:, :], ACT.Copy).then_inc(q_copied, 1)
                act.activation(qsqT[:, wide(g)], ps_q[:, :], ACT.Square).then_inc(q_copied, 1)
                for b in range(g * BPG, (g + 1) * BPG):
                    act.wait_ge(kv_done, b + 1)
                    src = ps_kv[b % 2][:, :].rearrange("p (t c) -> p t c", t=TPB)
                    act.activation(ksq[:, img(b), :], src[:, :, 0:C], ACT.Square).then_inc(kv_copied, 1)
                    act.activation(kv[:, img(b), :], src, ACT.Copy).then_inc(kv_copied, 1)

            def attend(g):
                act.wait_ge(qss_done, g + 1)
                act.activation(std_qk[:, tiles(g), 0:HEADS],
                               ps_qss.rearrange("p (t h) -> p t h", h=HEADS)[:, tiles(g), :],
                               ACT.Sqrt, bias=eps[:, 1:2], scale=1.0 / DH)
                act.wait_ge(kss_ready, g + 1)
                act.activation(std_qk[:, tiles(g), HEADS:2 * HEADS], kss[:, tiles(g), :],
                               ACT.Sqrt, bias=eps[:, 1:2], scale=1.0 / DH).then_inc(stdqk_ready, 1)
                for b in range(g * BPG, (g + 1) * BPG):
                    act.wait_ge(d_done, b + 1)
                    act.activation(beta_v[:, b, :], ps_d[:, P:2 * P],
                                   ACT.Copy).then_inc(betav_ready, 1)

            def norm2(g):
                act.wait_ge(var2_ready, g + 1)
                act.activation(std2[:, tiles(g)], mv2[:, tiles(g), 1], ACT.Sqrt, bias=eps[:, 1:2]).then_inc(std2_ready, 1)
                act.wait_ge(T2_done, g + 1)
                act.activation(x2T[:, wide(g)], ps_T[g % 2][:, :], ACT.Copy).then_inc(T2_copied, 1)

            for step in range(NG + 2):
                if step < NG:
                    norm(step)
                    project(step)
                if 0 <= step - 1 < NG:
                    attend(step - 1)
                if 0 <= step - 2 < NG:
                    norm2(step - 2)

            act.wait_ge(shifted_ready, 1)
            act.activation(expd[:, :, :], shifted[:, :, :], ACT.Exp).then_inc(exp_ready, 1)

            for e in range(E):
                for c in range(HC):
                    act.wait_ge(h_done, HC * e + c + 1)
                    if e >= 2 and c == 0:
                        act.wait_ge(y_done, e - 1)
                    act.activation(hid[:, e % 2, c, :], ps_h[c][:, 0:CAP], ACT.Gelu,
                                   bias=b1T[:, e * HC + c:e * HC + c + 1]).then_inc(h_ready, 1)

        @block.vector
        def _(dve):
            steps = [0]

            def link(ins):
                steps[0] += 1
                ins.then_inc(dve_step, 1)
                dve.wait_ge(dve_step, steps[0])

            dve.wait_ge(wqkv_in, 16)
            wv = wqkv[:, 0:2 * C].rearrange("p (h d) -> p h d", d=DH)
            dve.tensor_copy(w_c[:, 2 * C:3 * C], wqkv[:, 2 * C:3 * C])
            link(dve.tensor_reduce(w_sum[:, :], wv, AX, ALU.add))
            dve.scalar_tensor_tensor(w_c[:, 0:2 * C].rearrange("p (h d) -> p h d", d=DH),
                                     w_sum[:, :].unsqueeze(2).broadcast_to([C, 2 * HEADS, DH]), -1.0 / DH, wv,
                                     ALU.mult, ALU.add).then_inc(wc_ready, 1)
            dve.wait_ge(vecs_in, 64)
            for k in range(4):
                ins = dve.tensor_copy(vec_rows[:, k, :, :], vecs[:, k, :].unsqueeze(1).broadcast_to([P, HEADS, DH]))
            ins.then_inc(vec_ready, 1)
            dve.wait_ge(const_ready, 1)
            link(dve.tensor_scalar(diff[:, :], diff[:, :], E - 1, None, ALU.bitwise_and))
            dve.tensor_scalar(same_e[:, :], diff[:, :], 0.0, None, ALU.is_equal).then_inc(same_ready, 1)

            def norm(g):
                dve.wait_ge(x_in[g], 16)
                for t in range(g * GROUP, (g + 1) * GROUP):
                    ins = dve.bn_stats(stat[:, t, :], x_sb[:, t, :])
                link(ins)
                for t in range(g * GROUP, (g + 1) * GROUP):
                    ins = dve.bn_aggr(mv[:, t, :], stat[:, t, :])
                ins.then_inc(var_ready, 1)
                dve.wait_ge(std_ready, g + 1)
                link(dve.reciprocal(rstd[:, tiles(g)], std[:, tiles(g)]))
                for t in range(g * GROUP, (g + 1) * GROUP):
                    dve.tensor_scalar(xn[:, t, :], x_sb[:, t, :], mv[:, t, 0:1], rstd[:, t:t + 1],
                                      ALU.subtract, ALU.mult).then_inc(xn_ready, 1)

            def attend(g):
                dve.wait_ge(kv_copied, 2 * BPG * (g + 1))
                dve.tensor_reduce(kss[:, tiles(g), :], ksq[:, tiles(g), :].rearrange("p t (h d) -> p t h d", d=DH),
                                  AX, ALU.add).then_inc(kss_ready, 1)
                dve.wait_ge(stdqk_ready, g + 1)
                dve.reciprocal(r_qk[:, tiles(g), :], std_qk[:, tiles(g), :]).then_inc(rqk_ready, 1)
                for b in range(g * BPG, (g + 1) * BPG):
                    dve.wait_ge(betav_ready, b + 1)
                    link(dve.scalar_tensor_tensor(dots[:, b, :], ps_d[:, 0:P],
                                                  gamma_col[:, 1:2], beta_v[:, b, :], ALU.mult, ALU.add))
                    dve.tensor_tensor(dots_b[:, b, :], dots[:, b, :], head_mean[:, :], ALU.mult).then_inc(dots_ready, 1)
                    dve.scalar_tensor_tensor(dots_q[:, b, :], dots[:, b, :], gamma_col[:, 0:1], head_mean[:, :],
                                             ALU.mult, ALU.mult).then_inc(dotsq_ready, 1)
                    dve.wait_ge(rqk_ready, g + 1)
                    dve.wait_ge(o_done, b + 1)
                    dve.tensor_tensor(att[:, img(b), :].rearrange("p t (h d) -> p t h d", d=DH),
                                      ps_o[:, 0:TPB * P].rearrange("p (t h d) -> p t h d", h=HEADS, d=DH),
                                      r_qk[:, img(b), 0:HEADS].unsqueeze(3).broadcast_to([P, TPB, HEADS, DH]), ALU.mult)
                    dve.tensor_tensor(xb[:, img(b), :], x_sb[:, img(b), :],
                                      ps_o[:, TPB * P:TPB * P + P].unsqueeze(1).broadcast_to([P, TPB, P]),
                                      ALU.add).then_inc(o_used, 1)

            def norm2(g):
                dve.wait_ge(x1_ready, BPG * (g + 1))
                for t in range(g * GROUP, (g + 1) * GROUP):
                    ins = dve.bn_stats(stat2[:, t, :], x1[:, t, :])
                link(ins)
                for t in range(g * GROUP, (g + 1) * GROUP):
                    ins = dve.bn_aggr(mv2[:, t, :], stat2[:, t, :])
                ins.then_inc(var2_ready, 1)
                dve.wait_ge(std2_ready, g + 1)
                link(dve.reciprocal(rstd2[:, tiles(g)], std2[:, tiles(g)]))
                for t in range(g * GROUP, (g + 1) * GROUP):
                    dve.tensor_scalar(rows[:, t, 0:C], x1[:, t, :], mv2[:, t, 0:1], rstd2[:, t:t + 1],
                                      ALU.subtract, ALU.mult).then_inc(x2_ready, 1)

            for step in range(NG + 2):
                if step < NG:
                    norm(step)
                if step == 0:
                    dve.wait_ge(small_T, 1)
                    dve.tensor_copy(gamma_col[:, 0:1], ps_small[:, 0:1])
                    dve.tensor_copy(gamma_col[:, 1:2], ps_small[:, 1:2])
                    dve.tensor_copy(gateT[:, :], ps_small[:, 8:8 + E])
                    dve.tensor_copy(b1T[:, :], ps_small[:, 32:32 + E * HC])
                    link(dve.tensor_copy(qbeta_mat[:, :], ps_small[:, 128:256]))
                    dve.sem_inc(small_ready, 1)
                if 0 <= step - 1 < NG:
                    attend(step - 1)
                if 0 <= step - 2 < NG:
                    norm2(step - 2)

            def per_tile(s):
                return s[:, :].unsqueeze(2).broadcast_to([P, NT, E])

            dve.wait_ge(logit_done, NG)
            dve.wait_ge(gate_in, 32)
            link(dve.tensor_tensor(logit[:, :, :], ps_logit.rearrange("p (t e) -> p t e", e=E),
                                   gate_bias[:, :].unsqueeze(1).broadcast_to([P, NT, E]), ALU.add))
            link(dve.tensor_reduce(s1[:, :], logit[:, :, :], AX, ALU.max))
            dve.tensor_tensor(shifted[:, :, :], logit[:, :, :], per_tile(s1), ALU.subtract).then_inc(shifted_ready, 1)
            dve.wait_ge(exp_ready, 1)
            link(dve.tensor_reduce(s2[:, :], expd[:, :, :], AX, ALU.add))
            link(dve.reciprocal(s3[:, :], s2[:, :]))
            link(dve.tensor_tensor(prob[:, :, :], expd[:, :, :], per_tile(s3), ALU.mult))
            link(dve.tensor_reduce(s1[:, :], prob[:, :, :], AX, ALU.max))
            link(dve.tensor_tensor(g1[:, :, :], prob[:, :, :], per_tile(s1), ALU.is_lt))
            dve.tensor_reduce(s2[:, :], g1[:, :, :], AX, ALU.add)
            link(dve.tensor_tensor(g2[:, :, :], prob[:, :, :], g1[:, :, :], ALU.mult))
            link(dve.tensor_reduce(s3[:, :], g2[:, :, :], AX, ALU.max))
            link(dve.scalar_tensor_tensor(s4[:, :], s2[:, :], float(E - TOPK), s1[:, :], ALU.is_le, ALU.mult))
            link(dve.tensor_tensor(s4[:, :], s4[:, :], s3[:, :], ALU.max))
            link(dve.tensor_tensor(g1[:, :, :], prob[:, :, :], per_tile(s4), ALU.is_gt))
            dve.tensor_tensor(g2[:, :, :], prob[:, :, :], per_tile(s4), ALU.is_equal)
            link(dve.tensor_reduce(s5[:, :], g1[:, :, :], AX, ALU.add))
            link(dve.tensor_tensor_scan(g3[:, :, :].rearrange("p t e -> p (t e)"), expert_run[:, :],
                                        g2[:, :, :].rearrange("p t e -> p (t e)"), 0.0, ALU.mult, ALU.add))
            link(dve.tensor_tensor(g3[:, :, :], g3[:, :, :], per_tile(s5), ALU.add))
            link(dve.scalar_tensor_tensor(g4[:, :, :], g3[:, :, :], float(TOPK), g2[:, :, :], ALU.is_le, ALU.mult))
            link(dve.tensor_tensor(g4[:, :, :], g4[:, :, :], g1[:, :, :], ALU.add))
            link(dve.tensor_tensor(g3[:, :, :], g4[:, :, :], prob[:, :, :], ALU.mult))
            dve.tensor_copy(rows[:, :, C:ROW], g3[:, :, :]).then_inc(routed_ready, 1)

            dve.wait_ge(wT_done, 1)
            dve.memset(best[:, 0, 0:1], 0.0)
            link(dve.tensor_copy(wT[:, :], ps_small[:, 0:P]))
            for r in range(ROUNDS):
                shift = BITS - DIGIT * (r + 1)
                c = cand[:, r % 2, :]
                link(dve.tensor_scalar(c, digits[:, :], shift, best[:, r % 2, 0:1].bitcast(I32),
                                       ALU.logical_shift_left, ALU.bitwise_or))
                for j in range(CAND):
                    ins = dve.tensor_scalar(hits[:, j, :], wT[:, :], c[:, j:j + 1].bitcast(F32), None,
                                            ALU.is_ge, ALU.add, accum_out=count[:, r % 2, j:j + 1])
                ins.then_inc(counted, 1)
                dve.wait_ge(summed, r + 1)
                link(dve.scalar_tensor_tensor(best[:, r % 2, 1:1 + CAND], ps_cnt[:, 0:CAND], CAP - 0.5,
                                              c.bitcast(F32), ALU.is_ge, ALU.mult))
                link(dve.tensor_reduce(best[:, (r + 1) % 2, 0:1], best[:, r % 2, :], AX, ALU.max))
            thr = best[:, ROUNDS % 2, 0:1]
            dve.tensor_scalar(above[:, :], wT[:, :], thr, None, ALU.is_gt, ALU.add, accum_out=cnt2[:, 0:1])
            dve.tensor_scalar(level[:, :], wT[:, :], thr, None, ALU.is_equal, ALU.add,
                              accum_out=cnt2[:, 1:2]).then_inc(counted, 1)
            dve.wait_ge(summed, ROUNDS + 1)
            link(dve.tensor_copy(tot[:, :], ps_cnt[:, 0:4]))
            dve.tensor_scalar(need[:, :], tot[:, 0:1], -1.0, float(CAP), ALU.mult, ALU.add)
            dve.tensor_tensor_scan(run_above[:, :], above[:, :], zeros[:, :], tot[:, 2:3], ALU.add, ALU.add)
            link(dve.tensor_tensor_scan(run_level[:, :], level[:, :], zeros[:, :], tot[:, 3:4], ALU.add, ALU.add))
            link(dve.scalar_tensor_tensor(taken[:, :], run_level[:, :], need[:, :], level[:, :], ALU.is_le, ALU.mult))
            dve.tensor_tensor(taken[:, :], taken[:, :], above[:, :], ALU.add)
            link(dve.scalar_tensor_tensor(pos[:, :], run_level[:, :], need[:, :], run_above[:, :], ALU.min, ALU.add))
            dve.tensor_tensor(pos[:, :], pos[:, :], taken[:, :], ALU.mult).then_inc(pos_ready, 1)

            dve.wait_ge(slotT_done, 1)
            link(dve.tensor_scalar(slot[:, :], ps_small[:, P:2 * P], 1.0, None, ALU.subtract))
            dve.tensor_scalar(maj[:, :], slot[:, :], SUB.bit_length() - 1, MAJ - 1, ALU.logical_shift_right, ALU.bitwise_and)
            dve.tensor_scalar(mnr[:, :], slot[:, :], SUB - 1, None, ALU.bitwise_and)
            link(dve.tensor_scalar(chk[:, :], slot[:, :], 7, None, ALU.logical_shift_right))
            link(dve.tensor_scalar(chk[:, :], chk[:, :], SUB.bit_length() - 1, None, ALU.logical_shift_left))
            link(dve.tensor_tensor(cm[:, :], mnr[:, :], chk[:, :], ALU.bitwise_or))

            def onehots(e):
                def col(a, n):
                    return a[:, :].rearrange("p (t e) -> p t e", e=E)[:, :, e].unsqueeze(2).broadcast_to([P, NT, n])
                link(dve.tensor_tensor(oh_maj[:, e], col(maj, MAJ), iota_maj[:, :].unsqueeze(1).broadcast_to([P, NT, MAJ]),
                                       ALU.is_equal))
                dve.tensor_tensor(oh_tok[:, e], oh_maj[:, e], token_id[:, :].unsqueeze(2).broadcast_to([P, NT, MAJ]), ALU.mult)
                dve.tensor_tensor(oh_cm[:, e], col(cm, CM), iota_cm[:, :].unsqueeze(1).broadcast_to([P, NT, CM]),
                                  ALU.is_equal).then_inc(onehot_ready, 1)
                dve.wait_ge(grid_done, e + 1)
                dve.tensor_copy(grid[:, e, :], ps_grid[0:MAJ, 0:CM]).then_inc(grid_ready, 1)
                dve.wait_ge(index_done, e + 1)
                dve.tensor_copy(index[:, e, :], ps_grid[:, 64:64 + NC]).then_inc(index_ready, 1)

            def tokens_in(e):
                dve.wait_ge(xgT_done, e + 1)
                if e >= 2:
                    dve.wait_ge(h_done, HC * (e - 1))
                dve.tensor_copy(xgT[:, e % 2, :], ps_x[:, 0:CAP]).then_inc(xgT_ready, 1)

            def tokens_out(e):
                dve.wait_ge(y_done, e + 1)
                full = CAP // P
                last = CHUNKS[-1][1]
                dve.tensor_tensor(yb[:, e % 2, 0:full, :], ps_y[:, 0:full * C].rearrange("p (n c) -> p n c", c=C),
                                  b2_sb[:, e, :].unsqueeze(1).broadcast_to([P, full, C]), ALU.add)
                link(dve.tensor_tensor(yb[0:last, e % 2, full, :], ps_y[0:last, full * C:(full + 1) * C],
                                       b2_sb[0:last, e, :], ALU.add))
                dve.tensor_tensor(y[:, e, 0:full, :], yb[:, e % 2, 0:full, :],
                                  xg[:, e, 0:full, C + e:C + e + 1].broadcast_to([P, full, C]), ALU.mult)
                dve.tensor_scalar(y[0:last, e, full, :], yb[0:last, e % 2, full, :], xg[0:last, e, full, C + e:C + e + 1],
                                  None, ALU.mult).then_inc(y_ready, 1)

            dve.wait_ge(b_in, 32)
            onehots(0)
            onehots(1)
            tokens_in(0)
            for e in range(E):
                if e + 2 < E:
                    onehots(e + 2)
                if e + 1 < E:
                    tokens_in(e + 1)
                tokens_out(e)

        @block.tensor
        def _(pe):
            pe.wait_ge(const_ready, 1)
            pe.wait_ge(vec_ready, 1)
            pe.wait_ge(gate_in, 32)
            pe.wait_ge(b_in, 32)
            vr = vec_rows[:, :, :, :].rearrange("p k h d -> p k (h d)")
            pe.transpose(ps_small[:, 0:1], vr[0:1, 0, :], ident[0:1, 0:1])
            pe.transpose(ps_small[:, 1:2], vr[0:1, 2, :], ident[0:1, 0:1])
            pe.transpose(ps_small[:, 8:8 + E], gate_rows[:, :], ident[0:E, 0:E])
            pe.transpose(ps_small[:, 32:32 + E * HC], b1_rows[:, :], ident[0:E * HC, 0:E * HC])
            pe.transpose(ps_small[:, 128:256], vr[:, 1, :], ident[:, :]).then_inc(small_T, 1)

            def norm(g):
                if g >= 2:
                    pe.wait_ge(T_copied, g - 1)
                for i in range(GROUP):
                    t = g * GROUP + i
                    pe.wait_ge(xn_ready, t + 1)
                    ins = pe.transpose(ps_T[g % 2][:, i * P:(i + 1) * P], xn[:, t, :], ident[:, :])
                ins.then_inc(T_done, 1)

            def project(g):
                pe.wait_ge(T_copied, g + 1)
                if g == 0:
                    pe.wait_ge(wc_ready, 1)
                else:
                    pe.wait_ge(q_copied, 2 * g)
                pe.matmul(ps_q[:, :], w_c[:, 0:C], xnT[:, wide(g)], start=True, stop=True).then_inc(q_done, 1)
                for b in range(g * BPG, (g + 1) * BPG):
                    if b >= 2:
                        pe.wait_ge(kv_copied, 2 * (b - 1))
                    for i in range(TPB):
                        t = b * TPB + i
                        ins = pe.matmul(ps_kv[b % 2][:, i * 2 * C:(i + 1) * 2 * C], xnT[:, t * P:(t + 1) * P],
                                        w_c[:, C:3 * C], start=True, stop=True)
                    ins.then_inc(kv_done, 1)

            def attend(g):
                pe.wait_ge(q_copied, 2 * (g + 1))
                if g == 0:
                    pe.wait_ge(small_ready, 1)
                else:
                    pe.wait_ge(stdqk_ready, g)
                for t in range(g * GROUP, (g + 1) * GROUP):
                    ins = pe.matmul(ps_qss[:, t * HEADS:(t + 1) * HEADS], qsqT[:, t * P:(t + 1) * P],
                                    head_mask[:, ::DH], start=True, stop=True)
                ins.then_inc(qss_done, 1)
                for b in range(g * BPG, (g + 1) * BPG):
                    pe.wait_ge(kn_ready, b + 1)
                    if b >= 1:
                        pe.wait_ge(dotsq_ready, b)
                    for i in range(TPB):
                        t = b * TPB + i
                        pe.matmul(ps_d[:, 0:P], kn[:, t, :], kv[:, t, C:2 * C], start=(i == 0), stop=(i == TPB - 1))
                    for i in range(TPB):
                        t = b * TPB + i
                        ins = pe.matmul(ps_d[:, P:2 * P], vr[:, 3, :], kv[:, t, C:2 * C],
                                        start=(i == 0), stop=(i == TPB - 1))
                    ins.then_inc(d_done, 1)
                    pe.wait_ge(dotsq_ready, b + 1)
                    if b >= 1:
                        pe.wait_ge(o_used, b)
                    for i in range(TPB):
                        t = b * TPB + i
                        pe.matmul(ps_o[:, i * P:(i + 1) * P], qT[:, t * P:(t + 1) * P], dots_q[:, b, :],
                                  start=True, stop=True)
                    pe.matmul(ps_o[:, TPB * P:TPB * P + P], qbeta_mat[:, :], dots_b[:, b, :],
                              start=True, stop=True).then_inc(o_done, 1)

            def norm2(g):
                pe.wait_ge(T_copied, min(NG, g + 3))
                if g >= 2:
                    pe.wait_ge(T2_copied, g - 1)
                for i in range(GROUP):
                    t = g * GROUP + i
                    pe.wait_ge(x2_ready, t + 1)
                    ins = pe.transpose(ps_T[g % 2][:, i * P:(i + 1) * P], rows[:, t, 0:C], ident[:, :])
                ins.then_inc(T2_done, 1)
                pe.wait_ge(T2_copied, g + 1)
                pe.wait_ge(stdqk_ready, min(NG, g + 2))
                for t in range(g * GROUP, (g + 1) * GROUP):
                    ins = pe.matmul(ps_logit[:, t * E:(t + 1) * E], x2T[:, t * P:(t + 1) * P], gateT[:, :],
                                    start=True, stop=True)
                ins.then_inc(logit_done, 1)

            for step in range(NG + 2):
                if step < NG:
                    norm(step)
                    project(step)
                if 0 <= step - 1 < NG:
                    attend(step - 1)
                if 0 <= step - 2 < NG:
                    norm2(step - 2)

            pe.wait_ge(routed_ready, 1)
            pe.transpose(ps_small[:, 0:P], g3[:, :, :].rearrange("p t e -> p (t e)"), ident[:, :]).then_inc(wT_done, 1)
            pe.wait_ge(same_ready, 1)
            for r in range(ROUNDS):
                pe.wait_ge(counted, r + 1)
                pe.matmul(ps_cnt[:, 0:CAND], same_e[:, :], count[:, r % 2, :], start=True, stop=True).then_inc(summed, 1)
            pe.wait_ge(counted, ROUNDS + 1)
            pe.wait_ge(before_ready, 1)
            pe.matmul(ps_cnt[:, 0:2], same_e[:, :], cnt2[:, :], start=True, stop=True)
            pe.matmul(ps_cnt[:, 2:4], before_e[:, :], cnt2[:, :], start=True, stop=True).then_inc(summed, 1)
            pe.wait_ge(pos_ready, 1)
            pe.transpose(ps_small[:, P:2 * P], pos[:, :], ident[:, :]).then_inc(slotT_done, 1)

            def find_tokens(e):
                pe.wait_ge(onehot_ready, e + 1)
                if e >= 1:
                    pe.wait_ge(index_ready, e)
                for t in range(NT):
                    ins = pe.matmul(ps_grid[0:MAJ, 0:CM], oh_tok[:, e, t, :], oh_cm[:, e, t, :],
                                    start=(t == 0), stop=(t == NT - 1))
                ins.then_inc(grid_done, 1)
                pe.wait_ge(grid_ready, e + 1)
                for b in range(SUB):
                    ins = pe.matmul(ps_grid[:, 64:64 + NC], spread[:, b, :],
                                    grid[:, e, :].rearrange("a (c b) -> a c b", b=SUB)[:, :, b],
                                    start=(b == 0), stop=(b == SUB - 1))
                ins.then_inc(index_done, 1)

            def tokens_in(e):
                pe.wait_ge(gathered[e], 16 * NC)
                if e >= 1:
                    pe.wait_ge(xgT_ready, e)
                for c, (at, n) in enumerate(CHUNKS):
                    ins = pe.transpose(ps_x[:, at:at + n], xg[0:n, e, c, 0:C], ident[0:n, 0:n])
                ins.then_inc(xgT_done, 1)

            def up(e):
                pe.wait_ge(xgT_ready, e + 1)
                for c in range(HC):
                    if e >= 1:
                        pe.wait_ge(h_ready, HC * (e - 1) + c + 1)
                    pe.matmul(ps_h[c][:, 0:CAP], w1_sb[:, e, c * P:(c + 1) * P], xgT[:, e % 2, :],
                              start=True, stop=True).then_inc(h_done, 1)

            def down(e):
                pe.wait_ge(h_ready, HC * (e + 1))
                if e >= 1:
                    pe.wait_ge(y_ready, e)
                for k, (at, n) in enumerate(CHUNKS):
                    for c in range(HC):
                        ins = pe.matmul(ps_y[0:n, k * C:(k + 1) * C], hid[:, e % 2, c, at:at + n], w2_sb[:, e, c, :],
                                        start=(c == 0), stop=(c == HC - 1))
                ins.then_inc(y_done, 1)

            find_tokens(0)
            find_tokens(1)
            pe.wait_ge(w1_in, 16)
            pe.wait_ge(w2_in, 16)
            tokens_in(0)
            up(0)
            for e in range(E):
                if e + 2 < E:
                    find_tokens(e + 2)
                if e + 1 < E:
                    tokens_in(e + 1)
                    up(e + 1)
                down(e)


_INS = ['x', 'L0_conv_w_qkv', 'L0_conv_q_gamma', 'L0_conv_q_beta', 'L0_conv_k_gamma', 'L0_conv_k_beta',
        'L0_ffn_gate_w', 'L0_ffn_gate_b', 'L0_ffn_w1', 'L0_ffn_b1', 'L0_ffn_w2', 'L0_ffn_b2']


def kernel(**inputs):
    import numpy as _np
    import concourse.bacc as _bacc
    from concourse import mybir as _mybir
    from concourse.bass_utils import run_bass_kernel_spmd as _run

    nc = _bacc.Bacc("TRN2", target_bir_lowering=False, num_devices=1)
    arrays, args = {}, []
    for name in _INS:
        a = _np.ascontiguousarray(inputs[name])
        arrays[f"in_{name}_dram"] = a
        args.append(nc.dram_tensor(f"in_{name}_dram", a.shape, _mybir.dt.from_np(a.dtype), kind="ExternalInput").ap())
    shape = inputs['x'].shape
    out = nc.dram_tensor("out_0_dram", shape, _mybir.dt.float32, kind="ExternalOutput").ap()
    build(nc, *args, out)
    r = _run(nc, [arrays], core_ids=[0])
    return r.results[0]["out_0_dram"]
```

```python
from contextlib import ExitStack

import numpy as np

import concourse.bass as bass
from concourse import mybir

F32 = mybir.dt.float32
F16 = mybir.dt.float16
BF16 = mybir.dt.bfloat16
I32 = mybir.dt.int32
U32 = mybir.dt.uint32
ALU = mybir.AluOpType
ACT = mybir.ActivationFunctionType
AX = mybir.AxisListType.X

P = 128
HEADS, DH = 8, 16
TOPK = 2
CAP_FACTOR = 1.2
LN_C_EPS, LN_H_EPS, LN_T_EPS = 1e-6, 1e-5, 1e-5
DIGIT = 3
BITS = 30


def build(nc, x, w_qkv, q_gamma, q_beta, k_gamma, k_beta, gate_w, gate_b, w1, b1, w2, b2, out):
    B, L, W, C = x.shape
    N = L * W
    T = B * N
    E, _, HID = w1.shape
    NT = T // P
    TPB = N // P
    HC = HID // P
    CAP = int(CAP_FACTOR * T / E)
    CHUNKS = [(c * P, min(P, CAP - c * P)) for c in range(-(-CAP // P))]
    NC = len(CHUNKS)
    TE = NT * E
    ROW = C + E
    SUB = 8
    MAJ = P // SUB
    CM = NC * SUB
    CAND = 2 ** DIGIT - 1
    ROUNDS = BITS // DIGIT
    LEAD = 3
    assert C == P and TE == P and HEADS * DH == C

    x_d = x.rearrange("b l w c -> (b l w) c").rearrange("(t p) c -> p t c", p=P)
    out_rows = out.rearrange("b l w c -> (b l w) c")
    out_d = out_rows.rearrange("(t p) c -> p t c", p=P)
    table = nc.dram_tensor("table", [T, ROW], F32, kind="Internal").ap()
    table_d = table.rearrange("(t p) c -> p t c", p=P)

    with ExitStack() as ctx:
        def sb(name, shape, dt=F32):
            return ctx.enter_context(nc.sbuf_tensor(name, shape, dt))

        def sem(name):
            return ctx.enter_context(nc.semaphore(name))

        x_sb = sb("x_sb", [P, NT, C])
        wqkv = sb("wqkv", [C, 3 * C])
        vecs = sb("vecs", [P, 4, DH])
        gate_rows = sb("gate_rows", [E, C])
        gate_bias = sb("gate_bias", [P, E])
        b1_rows = sb("b1_rows", [E * HC, P])
        b2_sb = sb("b2_sb", [P, E, C])
        w1_sb = sb("w1_sb", [C, E, HID])
        w2_sb = sb("w2_sb", [P, E, HC, C])
        ident = sb("ident", [P, P])
        ones = sb("ones", [P, P])
        head_mask = sb("head_mask", [P, P])
        head_mean = sb("head_mean", [P, P])
        diff = sb("diff", [P, P], I32)
        same_e = sb("same_e", [P, P], BF16)
        before_e = sb("before_e", [P, P], BF16)
        token_id = sb("token_id", [P, NT])
        iota_maj = sb("iota_maj", [P, MAJ])
        iota_cm = sb("iota_cm", [P, CM])
        digits = sb("digits", [P, CAND], I32)
        expert_run = sb("expert_run", [P, TE])
        spread = sb("spread", [MAJ, SUB, P], F16)
        eps = sb("eps", [P, 2])
        zero1 = sb("zero1", [P, 1])
        col_mean = sb("col_mean", [P, P])
        w_h = sb("w_h", [C, 3 * C])
        w_c = sb("w_c", [C, 3 * C])
        w_sum = sb("w_sum", [C, 2 * HEADS])
        vec_rows = sb("vec_rows", [P, 4, HEADS, DH])
        head_mean_q = sb("head_mean_q", [P, P])
        qbeta_mat = sb("qbeta_mat", [P, P])
        stat = sb("stat", [P, NT, 6])
        mv = sb("mv", [P, NT, 2])
        eps_var = sb("eps_var", [P, NT])
        std = sb("std", [P, NT])
        rstd = sb("rstd", [P, NT])
        xT = sb("xT", [C, T])
        q_work = sb("q_work", [P, 2, T])
        qT, qsqT = q_work[:, 0, :], q_work[:, 1, :]
        kv = sb("kv", [P, NT, 2 * C])
        ksq = sb("ksq", [P, NT, C])
        kss = sb("kss", [P, NT, HEADS])
        k_var = sb("k_var", [P, NT, HEADS])
        k_std = sb("k_std", [P, NT, HEADS])
        k_rstd = sb("k_rstd", [P, NT, HEADS])
        q_var = sb("q_var", [P, NT, HEADS])
        q_std = sb("q_std", [P, NT, HEADS])
        q_rstd = sb("q_rstd", [P, NT, HEADS])
        kn = ksq
        dots_b = sb("dots_b", [P, B, P])
        dots_q = sb("dots_q", [P, B, P])
        att = sb("att", [P, NT, C])
        xb = sb("xb", [P, NT, C])
        x1 = att
        stat2 = sb("stat2", [P, NT, 6])
        mv2 = sb("mv2", [P, NT, 2])
        std2 = sb("std2", [P, NT])
        rstd2 = sb("rstd2", [P, NT])
        rows = sb("rows", [P, NT, ROW])
        x1T = xT
        shift2 = sb("shift2", [P, NT])
        gate_c = sb("gate_c", [E, C])
        gate_sum = sb("gate_sum", [E, 1])
        gateT = sb("gateT", [C, E])
        b1T = sb("b1T", [P, E * HC])
        logit = sb("logit", [P, NT, E])
        shifted = sb("shifted", [P, NT, E])
        expd = sb("expd", [P, NT, E])
        prob = sb("prob", [P, NT, E])
        g1 = sb("g1", [P, NT, E])
        g2 = sb("g2", [P, NT, E])
        g3 = sb("g3", [P, NT, E])
        g4 = sb("g4", [P, NT, E])
        s1 = sb("s1", [P, NT])
        s2 = sb("s2", [P, NT])
        s3 = sb("s3", [P, NT])
        s4 = sb("s4", [P, NT])
        s5 = sb("s5", [P, NT])
        wT = sb("wT", [TE, P])
        cand = sb("cand", [TE, 2, CAND], I32)
        hits = sb("hits", [TE, CAND, P], BF16)
        count = sb("count", [TE, 2, CAND], BF16)
        best = sb("best", [TE, 2, CAND + 1])
        above = sb("above", [TE, P])
        level = sb("level", [TE, P])
        cnt2 = sb("cnt2", [TE, 2], BF16)
        tot = sb("tot", [TE, 4])
        need = sb("need", [TE, 1])
        run_above = sb("run_above", [TE, P])
        run_level = sb("run_level", [TE, P])
        zeros = sb("zeros", [TE, P])
        ones_te = ones
        taken = sb("taken", [TE, P])
        pos = sb("pos", [TE, P])
        slot_f = sb("slot_f", [P, TE])
        slot = sb("slot", [P, TE], I32)
        maj = sb("maj", [P, TE], I32)
        mnr = sb("mnr", [P, TE], I32)
        chk = sb("chk", [P, TE], I32)
        cm = sb("cm", [P, TE], I32)
        oh_maj = sb("oh_maj", [P, E, NT, MAJ], F16)
        oh_tok = sb("oh_tok", [P, E, NT, MAJ], F16)
        oh_cm = sb("oh_cm", [P, E, NT, CM], F16)
        grid = sb("grid", [MAJ, E, CM], F16)
        index = sb("index", [P, E, NC], U32)
        xg = kv[:, :, :].rearrange("p t c -> p (t c)")[:, 0:E * NC * ROW].rearrange(
            "p (e n r) -> p e n r", e=E, n=NC)
        xgT = sb("xgT", [C, 2, CAP])
        hid = sb("hid", [P, 2, HC, CAP])
        yb = sb("yb", [P, 2, NC, C])
        y = q_work[:, :, :].rearrange("p a t -> p (a t)")[:, 0:E * NC * C].rearrange(
            "p (e n c) -> p e n c", e=E, n=NC)

        banks = [ctx.enter_context(nc.psum_tensor(f"bank{i}", [P, 512], F32)) for i in range(8)]
        ps_T, ps_q, ps_kv, ps_d, ps_o, ps_T1, ps_qss, misc = banks
        ps_logit = misc[:, 0:TE]
        ps_small = misc[:, 256:512]
        ps_h = [banks[1], banks[2], banks[3], banks[4]]
        ps_x = banks[0]
        ps_y = banks[5]
        ps_grid = banks[6]
        ps_cnt = banks[7]

        x_in = [sem(f"x_in{b}") for b in range(B)]
        wqkv_in, vecs_in, gate_in, b_in, w1_in, w2_in = (sem(n) for n in (
            "wqkv_in", "vecs_in", "gate_in", "b_in", "w1_in", "w2_in"))
        pool_step, dve_step = sem("pool_step"), sem("dve_step")
        ident_ready, const_ready, same_ready, before_ready = (
            sem("ident_ready"), sem("const_ready"), sem("same_ready"), sem("before_ready"))
        wh_ready, wmean_done, wc_ready, vec_ready, gatec_ready = (
            sem("wh_ready"), sem("wmean_done"), sem("wc_ready"), sem("vec_ready"), sem("gatec_ready"))
        small_T, small_ready, b1T_done = sem("small_T"), sem("small_ready"), sem("b1T_done")
        var_ready, std_ready, rstd_ready = sem("var_ready"), sem("std_ready"), sem("rstd_ready")
        T_done, T_copied = sem("T_done"), sem("T_copied")
        q_done, q_copied, kv_done, kv_copied = sem("q_done"), sem("q_copied"), sem("kv_done"), sem("kv_copied")
        kvar_ready, kstd_ready, krstd_ready, kn_ready = (
            sem("kvar_ready"), sem("kstd_ready"), sem("krstd_ready"), sem("kn_ready"))
        qss_done, qvar_ready, qstd_ready, qrstd_ready = (
            sem("qss_done"), sem("qvar_ready"), sem("qstd_ready"), sem("qrstd_ready"))
        d_done, dots_ready, o_done, o_used, x1_ready = (
            sem("d_done"), sem("dots_ready"), sem("o_done"), sem("o_used"), sem("x1_ready"))
        var2_ready, std2_ready, shift2_ready, x2_ready = (
            sem("var2_ready"), sem("std2_ready"), sem("shift2_ready"), sem("x2_ready"))
        T1_done, T1_copied, logit_done = sem("T1_done"), sem("T1_copied"), sem("logit_done")
        shifted_ready, exp_ready, routed_ready, wT_done = (
            sem("shifted_ready"), sem("exp_ready"), sem("routed_ready"), sem("wT_done"))
        counted, summed = sem("counted"), sem("summed")
        pos_ready, slotT_done = sem("pos_ready"), sem("slotT_done")
        onehot_ready, grid_done, grid_ready, index_done, index_ready = (
            sem("onehot_ready"), sem("grid_done"), sem("grid_ready"), sem("index_done"), sem("index_ready"))
        gathered = [sem(f"gathered{e}") for e in range(E)]
        xgT_done, xgT_ready, h_done, h_ready, y_done, y_ready = (
            sem("xgT_done"), sem("xgT_ready"), sem("h_done"), sem("h_ready"), sem("y_done"), sem("y_ready"))
        table_out, out_init = sem("table_out"), sem("out_init")
        added = [sem(f"added{e}") for e in range(E)]

        block = ctx.enter_context(nc.Block())

        def img(b):
            return slice(b * TPB, (b + 1) * TPB)

        def cols(b):
            return slice(b * N, (b + 1) * N)

        STEPS = B + 5

        def live(b):
            return 0 <= b < B

        @block.sync
        def _(sp):
            for b in range(B):
                sp.dma_start(x_sb[:, img(b), :], x_d[:, img(b), :]).then_inc(x_in[b], 16)
                if b == 1:
                    sp.dma_start(wqkv[:, :], w_qkv).then_inc(wqkv_in, 16)
            sp.dma_start(w1_sb[:, :, :], w1.rearrange("e c h -> c e h")).then_inc(w1_in, 16)
            sp.dma_start(w2_sb[:, :, :, :].rearrange("p e c d -> p (e c) d"),
                         w2.rearrange("e (c p) d -> p (e c) d", p=P)).then_inc(w2_in, 16)
            for b in range(B):
                sp.wait_ge(x1_ready, b + 1)
                sp.dma_start(out_d[:, img(b), :], x1[:, img(b), :]).then_inc(out_init, 16)
            sp.wait_ge(x2_ready, NT)
            sp.wait_ge(routed_ready, 1)
            sp.dma_start(table_d, rows[:, :, :]).then_inc(table_out, 16)
            sp.wait_ge(out_init, 16 * B)
            sp.wait_ge(table_out, 16)
            for e in range(E):
                sp.wait_ge(added[e], 16 * NC)

        @block.gpsimd
        def _(pool):
            steps = [0]

            def link(ins):
                steps[0] += 1
                ins.then_inc(pool_step, 1)
                pool.wait_ge(pool_step, steps[0])

            link(pool.memset(ident[:, :], 0.0))
            pool.affine_select(out=ident[:, :], in_=ident[:, :], compare_op=ALU.not_equal, fill=1.0,
                               base=0, pattern=[[-1, P]], channel_multiplier=1).then_inc(ident_ready, 1)
            pool.memset(eps[:, 0:1], LN_C_EPS)
            pool.memset(eps[:, 1:2], LN_H_EPS)
            pool.memset(col_mean[:, :], 1.0 / C)
            link(pool.memset(ones[:, :], 1.0))
            hm = head_mask[:, :].rearrange("p (h d) -> p h d", d=DH)
            link(pool.affine_select(out=hm, in_=ones[:, :].rearrange("p (h d) -> p h d", d=DH),
                                    compare_op=ALU.is_ge, fill=0.0, base=0,
                                    pattern=[[-DH, HEADS], [0, DH]], channel_multiplier=1))
            link(pool.affine_select(out=hm, in_=hm, compare_op=ALU.is_ge, fill=0.0, base=DH - 1,
                                    pattern=[[DH, HEADS], [0, DH]], channel_multiplier=-1))
            pool.tensor_scalar(head_mean[:, :], head_mask[:, :], 1.0 / N, None, ALU.mult).then_inc(const_ready, 1)

            def late_constants():
                pool.memset(zeros[:, :], 0.0)
                pool.memset(expert_run[:, :], 1.0)
                pool.iota(digits[:, :], [[1, CAND]], base=1, channel_multiplier=0)
                pool.iota(diff[:, :], [[-1, P]], base=P, channel_multiplier=1)
                pool.iota(token_id[:, :], [[P, NT]], base=0, channel_multiplier=1, allow_small_or_imprecise_dtypes=True)
                pool.iota(iota_maj[:, :], [[1, MAJ]], base=0, channel_multiplier=0, allow_small_or_imprecise_dtypes=True)
                pool.iota(iota_cm[:, :], [[1, CM]], base=0, channel_multiplier=0, allow_small_or_imprecise_dtypes=True)
                link(pool.memset(spread[:, :, :], 0.0))
                pool.memset(expert_run[:, :].rearrange("p (t e) -> p t e", e=E)[:, :, 0:1], 0.0)
                pool.affine_select(out=spread[:, :, :], in_=spread[:, :, :], compare_op=ALU.not_equal, fill=1.0,
                                   base=0, pattern=[[-1, SUB], [1, P]], channel_multiplier=-SUB).then_inc(const_ready, 1)

            def scale_k(b):
                def by_head(a):
                    return a.rearrange("p t (h d) -> p t h d", d=DH)
                pool.wait_ge(kv_copied, 4 * b + 2)
                pool.wait_ge(krstd_ready, b + 1)
                if b == 0:
                    pool.wait_ge(vec_ready, 1)
                link(pool.tensor_tensor(by_head(kn[:, img(b), :]), by_head(kv[:, img(b), 0:C]),
                                        k_rstd[:, img(b), :].unsqueeze(3).broadcast_to([P, TPB, HEADS, DH]), ALU.mult))
                pool.tensor_tensor(kn[:, img(b), :], kn[:, img(b), :],
                                   vec_rows[:, 2, :, :].rearrange("p h d -> p (h d)").unsqueeze(1).broadcast_to([P, TPB, C]),
                                   ALU.mult).then_inc(kn_ready, 1)

            def residual(b):
                pool.wait_ge(o_used, b + 1)
                pool.tensor_tensor(x1[:, img(b), :], att[:, img(b), :], xb[:, img(b), :], ALU.add).then_inc(x1_ready, 1)

            for s in range(STEPS):
                if live(s - 1):
                    scale_k(s - 1)
                if live(s - 3):
                    residual(s - 3)
            late_constants()
            pool.wait_ge(same_ready, 1)
            pool.affine_select(out=before_e[:, :], in_=same_e[:, :], compare_op=ALU.is_gt, fill=0.0,
                               base=0, pattern=[[1, P]], channel_multiplier=-1).then_inc(before_ready, 1)

            def gather(e):
                pool.wait_ge(index_ready, e + 1)
                if e == 0:
                    pool.wait_ge(table_out, 16)
                for c, (_, n) in enumerate(CHUNKS):
                    pool.indirect_dma_start(
                        out=xg[0:n, e, c, :], out_offset=None, in_=table,
                        in_offset=bass.IndirectOffsetOnAxis(ap=index[0:n, e, c:c + 1], axis=0)).then_inc(gathered[e], 16)

            def scatter(e):
                if e == 0:
                    pool.wait_ge(out_init, 16 * B)
                else:
                    pool.wait_ge(added[e - 1], 16 * NC)
                pool.wait_ge(y_ready, e + 1)
                for c, (_, n) in enumerate(CHUNKS):
                    pool.indirect_dma_start(
                        out=out_rows, out_offset=bass.IndirectOffsetOnAxis(ap=index[0:n, e, c:c + 1], axis=0),
                        in_=y[0:n, e, c, :], in_offset=None, compute_op=ALU.add).then_inc(added[e], 16)

            for e in range(LEAD):
                gather(e)
            for e in range(E):
                if e + LEAD < E:
                    gather(e + LEAD)
                scatter(e)

        @block.scalar
        def _(act):
            for k, v in enumerate((q_gamma, q_beta, k_gamma, k_beta)):
                act.dma_start(vecs[:, k, :], v.partition_broadcast(P)).then_inc(vecs_in, 16)
            act.dma_start(gate_rows[:, :], gate_w).then_inc(gate_in, 16)
            act.dma_start(gate_bias[:, :], gate_b.partition_broadcast(P)).then_inc(gate_in, 16)
            act.dma_start(b1_rows[:, :], b1.rearrange("e (c p) -> (e c) p", p=P)).then_inc(b_in, 16)
            act.dma_start(b2_sb[:, :, :].rearrange("p e c -> p (e c)"),
                          b2.rearrange("e c -> (e c)").partition_broadcast(P)).then_inc(b_in, 16)
            act.wait_ge(const_ready, 1)

            for s in range(STEPS):
                if live(s):
                    act.wait_ge(var_ready, s + 1)
                    act.activation(std[:, img(s)], mv[:, img(s), 1], ACT.Sqrt, bias=eps[:, 0:1]).then_inc(std_ready, 1)
                    act.wait_ge(T_done, s + 1)
                    act.activation(xT[:, cols(s)], ps_T[:, 0:N], ACT.Copy).then_inc(T_copied, 1)
                if live(s - 1):
                    act.wait_ge(kvar_ready, s)
                    act.activation(k_std[:, img(s - 1), :], k_var[:, img(s - 1), :], ACT.Sqrt,
                                   bias=zero1[:, :]).then_inc(kstd_ready, 1)
                if live(s):
                    act.wait_ge(q_done, s + 1)
                    act.activation(qsqT[:, cols(s)], ps_q[:, 0:N], ACT.Square).then_inc(q_copied, 1)
                    act.activation(qT[:, cols(s)], ps_q[:, 0:N], ACT.Copy).then_inc(q_copied, 1)
                if live(s - 1):
                    act.wait_ge(qvar_ready, s)
                    act.activation(q_std[:, img(s - 1), :], q_var[:, img(s - 1), :], ACT.Sqrt,
                                   bias=zero1[:, :]).then_inc(qstd_ready, 1)
                if live(s):
                    src = ps_kv[:, :].rearrange("p (t c) -> p t c", t=TPB)
                    act.wait_ge(kv_done, s + 1)
                    act.activation(ksq[:, img(s), :], src[:, :, 0:C], ACT.Square).then_inc(kv_copied, 1)
                    act.activation(kv[:, img(s), 0:C], src[:, :, 0:C], ACT.Copy).then_inc(kv_copied, 1)
                    act.wait_ge(rstd_ready, s + 1)
                    for i in range(TPB):
                        t = s * TPB + i
                        act.activation(kv[:, t, C:2 * C], src[:, i, C:2 * C], ACT.Copy,
                                       scale=rstd[:, t:t + 1]).then_inc(kv_copied, 1)
                if live(s - 4):
                    act.wait_ge(T1_done, s - 3)
                    act.activation(x1T[:, cols(s - 4)], ps_T1[:, 0:N], ACT.Copy).then_inc(T1_copied, 1)

            act.wait_ge(var2_ready, 1)
            act.activation(std2[:, :], mv2[:, :, 1], ACT.Sqrt, bias=eps[:, 1:2]).then_inc(std2_ready, 1)
            act.wait_ge(shifted_ready, 1)
            act.activation(expd[:, :, :], shifted[:, :, :], ACT.Exp).then_inc(exp_ready, 1)
            act.wait_ge(shift2_ready, 1)
            for t in range(NT):
                act.activation(rows[:, t, 0:C], x1[:, t, :], ACT.Identity, bias=shift2[:, t:t + 1],
                               scale=rstd2[:, t:t + 1]).then_inc(x2_ready, 1)

            for e in range(E):
                for c in range(HC):
                    act.wait_ge(h_done, HC * e + c + 1)
                    if e >= 2 and c == 0:
                        act.wait_ge(y_done, e - 1)
                    act.activation(hid[:, e % 2, c, :], ps_h[c][:, 0:CAP], ACT.Gelu,
                                   bias=b1T[:, e * HC + c:e * HC + c + 1]).then_inc(h_ready, 1)

        @block.vector
        def _(dve):
            steps = [0]

            def link(ins):
                steps[0] += 1
                ins.then_inc(dve_step, 1)
                dve.wait_ge(dve_step, steps[0])

            def stats(b):
                dve.wait_ge(x_in[b], 16)
                for t in range(b * TPB, (b + 1) * TPB):
                    ins = dve.bn_stats(stat[:, t, :], x_sb[:, t, :])
                link(ins)
                for t in range(b * TPB, (b + 1) * TPB):
                    ins = dve.bn_aggr(mv[:, t, :], stat[:, t, :])
                ins.then_inc(var_ready, 1)

            def stats_rest(b):
                dve.wait_ge(var_ready, b + 1)
                dve.tensor_scalar(eps_var[:, img(b)], mv[:, img(b), 1], LN_C_EPS, LN_H_EPS, ALU.add, ALU.mult)
                dve.wait_ge(std_ready, b + 1)
                dve.reciprocal(rstd[:, img(b)], std[:, img(b)]).then_inc(rstd_ready, 1)

            stats(0)
            dve.wait_ge(wqkv_in, 16)
            wv = wqkv[:, 0:2 * C].rearrange("p (h d) -> p h d", d=DH)
            dve.tensor_copy(w_h[:, 2 * C:3 * C], wqkv[:, 2 * C:3 * C])
            link(dve.tensor_reduce(w_sum[:, :], wv, AX, ALU.add))
            dve.scalar_tensor_tensor(w_h[:, 0:2 * C].rearrange("p (h d) -> p h d", d=DH),
                                     w_sum[:, :].unsqueeze(2).broadcast_to([C, 2 * HEADS, DH]), -1.0 / DH, wv,
                                     ALU.mult, ALU.add).then_inc(wh_ready, 1)
            dve.memset(zero1[:, :], 0.0)
            stats_rest(0)
            dve.wait_ge(wmean_done, 1)
            dve.tensor_tensor(w_c[:, :], w_h[:, :], ps_T1[:, 0:3 * C], ALU.subtract).then_inc(wc_ready, 1)
            dve.wait_ge(vecs_in, 64)
            for k in range(4):
                ins = dve.tensor_copy(vec_rows[:, k, :, :], vecs[:, k, :].unsqueeze(1).broadcast_to([P, HEADS, DH]))
            ins.then_inc(vec_ready, 1)
            dve.wait_ge(gate_in, 32)
            link(dve.tensor_reduce(gate_sum[:, :], gate_rows[:, :], AX, ALU.add))
            dve.scalar_tensor_tensor(gate_c[:, :], gate_sum[:, :].broadcast_to([E, C]), -1.0 / C, gate_rows[:, :],
                                     ALU.mult, ALU.add).then_inc(gatec_ready, 1)

            for s in range(STEPS):
                if live(s - 1):
                    b = s - 1
                    dve.wait_ge(kv_copied, 4 * b + 1)
                    link(dve.tensor_reduce(kss[:, img(b), :], ksq[:, img(b), :].rearrange("p t (h d) -> p t h d", d=DH),
                                           AX, ALU.add))
                    dve.scalar_tensor_tensor(k_var[:, img(b), :], kss[:, img(b), :], 1.0 / DH,
                                             eps_var[:, img(b)].unsqueeze(2).broadcast_to([P, TPB, HEADS]),
                                             ALU.mult, ALU.add).then_inc(kvar_ready, 1)
                if live(s) and s > 0:
                    stats(s)
                if live(s - 1):
                    dve.wait_ge(kstd_ready, s)
                    dve.reciprocal(k_rstd[:, img(s - 1), :], k_std[:, img(s - 1), :]).then_inc(krstd_ready, 1)
                if s == 1:
                    dve.wait_ge(small_T, 1)
                    dve.tensor_scalar(head_mean_q[:, :], head_mean[:, :], ps_small[:, 0:1], None, ALU.mult)
                    dve.tensor_copy(gateT[:, :], ps_small[:, 8:8 + E])
                    dve.tensor_copy(qbeta_mat[:, :], ps_small[:, 128:256]).then_inc(small_ready, 1)
                if live(s - 3):
                    b = s - 3
                    dve.wait_ge(qrstd_ready, b + 1)
                    dve.wait_ge(o_done, b + 1)
                    dve.tensor_tensor(att[:, img(b), :].rearrange("p t (h d) -> p t h d", d=DH),
                                      ps_o[:, 0:TPB * P].rearrange("p (t h d) -> p t h d", h=HEADS, d=DH),
                                      q_rstd[:, img(b), :].unsqueeze(3).broadcast_to([P, TPB, HEADS, DH]), ALU.mult)
                    dve.tensor_tensor(xb[:, img(b), :], x_sb[:, img(b), :],
                                      ps_o[:, TPB * P:TPB * P + P].unsqueeze(1).broadcast_to([P, TPB, P]),
                                      ALU.add).then_inc(o_used, 1)
                if live(s - 1):
                    b = s - 1
                    dve.wait_ge(qss_done, b + 1)
                    dve.scalar_tensor_tensor(q_var[:, img(b), :],
                                             ps_qss[:, 0:TPB * HEADS].rearrange("p (t h) -> p t h", h=HEADS), 1.0 / DH,
                                             eps_var[:, img(b)].unsqueeze(2).broadcast_to([P, TPB, HEADS]),
                                             ALU.mult, ALU.add).then_inc(qvar_ready, 1)
                if live(s - 2):
                    b = s - 2
                    if b == 0:
                        dve.wait_ge(small_ready, 1)
                    dve.wait_ge(d_done, b + 1)
                    dve.tensor_tensor(dots_b[:, b, :], ps_d[:, 0:P], head_mean[:, :], ALU.mult)
                    dve.tensor_tensor(dots_q[:, b, :], ps_d[:, 0:P], head_mean_q[:, :], ALU.mult).then_inc(dots_ready, 1)
                if live(s) and s > 0:
                    stats_rest(s)
                if live(s - 4):
                    b = s - 4
                    dve.wait_ge(x1_ready, b + 1)
                    for i in range(TPB):
                        ins = dve.bn_stats(stat2[:, b * TPB + i, :], x1[:, b * TPB + i, :])
                    link(ins)
                    for i in range(TPB):
                        ins = dve.bn_aggr(mv2[:, b * TPB + i, :], stat2[:, b * TPB + i, :])
                    if b == B - 1:
                        ins.then_inc(var2_ready, 1)
                if live(s - 1):
                    dve.wait_ge(qstd_ready, s)
                    dve.reciprocal(q_rstd[:, img(s - 1), :], q_std[:, img(s - 1), :]).then_inc(qrstd_ready, 1)

            dve.wait_ge(std2_ready, 1)
            link(dve.reciprocal(rstd2[:, :], std2[:, :]))

            def per_tile(s):
                return s[:, :].unsqueeze(2).broadcast_to([P, NT, E])

            dve.wait_ge(logit_done, B)
            link(dve.tensor_tensor(logit[:, :, :], ps_logit.rearrange("p (t e) -> p t e", e=E), per_tile(rstd2), ALU.mult))
            link(dve.tensor_tensor(logit[:, :, :], logit[:, :, :],
                                   gate_bias[:, :].unsqueeze(1).broadcast_to([P, NT, E]), ALU.add))
            link(dve.tensor_reduce(s1[:, :], logit[:, :, :], AX, ALU.max))
            dve.tensor_tensor(shifted[:, :, :], logit[:, :, :], per_tile(s1), ALU.subtract).then_inc(shifted_ready, 1)
            dve.scalar_tensor_tensor(shift2[:, :], mv2[:, :, 0], -1.0, rstd2[:, :], ALU.mult, ALU.mult).then_inc(shift2_ready, 1)
            dve.wait_ge(const_ready, 2)
            link(dve.tensor_scalar(diff[:, :], diff[:, :], E - 1, None, ALU.bitwise_and))
            dve.tensor_scalar(same_e[:, :], diff[:, :], 0.0, None, ALU.is_equal).then_inc(same_ready, 1)
            dve.wait_ge(b1T_done, 1)
            dve.tensor_copy(b1T[:, :], ps_T[:, 0:E * HC])
            dve.wait_ge(exp_ready, 1)
            link(dve.tensor_reduce(s2[:, :], expd[:, :, :], AX, ALU.add))
            link(dve.reciprocal(s3[:, :], s2[:, :]))
            link(dve.tensor_tensor(prob[:, :, :], expd[:, :, :], per_tile(s3), ALU.mult))
            link(dve.tensor_reduce(s1[:, :], prob[:, :, :], AX, ALU.max))
            link(dve.tensor_tensor(g1[:, :, :], prob[:, :, :], per_tile(s1), ALU.is_lt))
            dve.tensor_reduce(s2[:, :], g1[:, :, :], AX, ALU.add)
            link(dve.tensor_tensor(g2[:, :, :], prob[:, :, :], g1[:, :, :], ALU.mult))
            link(dve.tensor_reduce(s3[:, :], g2[:, :, :], AX, ALU.max))
            link(dve.scalar_tensor_tensor(s4[:, :], s2[:, :], float(E - TOPK), s1[:, :], ALU.is_le, ALU.mult))
            link(dve.tensor_tensor(s4[:, :], s4[:, :], s3[:, :], ALU.max))
            link(dve.tensor_tensor(g1[:, :, :], prob[:, :, :], per_tile(s4), ALU.is_gt))
            dve.tensor_tensor(g2[:, :, :], prob[:, :, :], per_tile(s4), ALU.is_equal)
            link(dve.tensor_reduce(s5[:, :], g1[:, :, :], AX, ALU.add))
            link(dve.tensor_tensor_scan(g3[:, :, :].rearrange("p t e -> p (t e)"), expert_run[:, :],
                                        g2[:, :, :].rearrange("p t e -> p (t e)"), 0.0, ALU.mult, ALU.add))
            link(dve.tensor_tensor(g3[:, :, :], g3[:, :, :], per_tile(s5), ALU.add))
            link(dve.scalar_tensor_tensor(g4[:, :, :], g3[:, :, :], float(TOPK), g2[:, :, :], ALU.is_le, ALU.mult))
            link(dve.tensor_tensor(g4[:, :, :], g4[:, :, :], g1[:, :, :], ALU.add))
            link(dve.tensor_tensor(g3[:, :, :], g4[:, :, :], prob[:, :, :], ALU.mult))
            dve.tensor_copy(rows[:, :, C:ROW], g3[:, :, :]).then_inc(routed_ready, 1)

            dve.wait_ge(wT_done, 1)
            dve.memset(best[:, 0, 0:1], 0.0)
            link(dve.tensor_copy(wT[:, :], ps_small[:, 0:P]))
            for r in range(ROUNDS):
                shift = BITS - DIGIT * (r + 1)
                c = cand[:, r % 2, :]
                link(dve.tensor_scalar(c, digits[:, :], shift, best[:, r % 2, 0:1].bitcast(I32),
                                       ALU.logical_shift_left, ALU.bitwise_or))
                for j in range(CAND):
                    ins = dve.tensor_scalar(hits[:, j, :], wT[:, :], c[:, j:j + 1].bitcast(F32), None,
                                            ALU.is_ge, ALU.add, accum_out=count[:, r % 2, j:j + 1])
                ins.then_inc(counted, 1)
                dve.wait_ge(summed, r + 1)
                link(dve.scalar_tensor_tensor(best[:, r % 2, 1:1 + CAND], ps_cnt[:, 0:CAND], CAP - 0.5,
                                              c.bitcast(F32), ALU.is_ge, ALU.mult))
                link(dve.tensor_reduce(best[:, (r + 1) % 2, 0:1], best[:, r % 2, :], AX, ALU.max))
            thr = best[:, ROUNDS % 2, 0:1]
            dve.tensor_scalar(above[:, :], wT[:, :], thr, None, ALU.is_gt, ALU.add, accum_out=cnt2[:, 0:1])
            dve.tensor_scalar(level[:, :], wT[:, :], thr, None, ALU.is_equal, ALU.add,
                              accum_out=cnt2[:, 1:2]).then_inc(counted, 1)
            dve.wait_ge(summed, ROUNDS + 1)
            link(dve.tensor_copy(tot[:, :], ps_cnt[:, 0:4]))
            dve.tensor_scalar(need[:, :], tot[:, 0:1], -1.0, float(CAP), ALU.mult, ALU.add)
            dve.tensor_tensor_scan(run_above[:, :], above[:, :], zeros[:, :], tot[:, 2:3], ALU.add, ALU.add)
            link(dve.tensor_tensor_scan(run_level[:, :], level[:, :], zeros[:, :], tot[:, 3:4], ALU.add, ALU.add))
            link(dve.scalar_tensor_tensor(taken[:, :], run_level[:, :], need[:, :], level[:, :], ALU.is_le, ALU.mult))
            dve.tensor_tensor(taken[:, :], taken[:, :], above[:, :], ALU.add)
            link(dve.scalar_tensor_tensor(pos[:, :], run_level[:, :], need[:, :], run_above[:, :], ALU.min, ALU.add))
            dve.tensor_tensor(pos[:, :], pos[:, :], taken[:, :], ALU.mult).then_inc(pos_ready, 1)

            dve.wait_ge(slotT_done, 1)
            link(dve.tensor_scalar(slot[:, :], ps_small[:, P:2 * P], 1.0, None, ALU.subtract))
            dve.tensor_scalar(maj[:, :], slot[:, :], SUB.bit_length() - 1, MAJ - 1, ALU.logical_shift_right, ALU.bitwise_and)
            dve.tensor_scalar(mnr[:, :], slot[:, :], SUB - 1, None, ALU.bitwise_and)
            link(dve.tensor_scalar(chk[:, :], slot[:, :], 7, None, ALU.logical_shift_right))
            link(dve.tensor_scalar(chk[:, :], chk[:, :], SUB.bit_length() - 1, None, ALU.logical_shift_left))
            link(dve.tensor_tensor(cm[:, :], mnr[:, :], chk[:, :], ALU.bitwise_or))

            def onehots(e):
                def col(a, n):
                    return a[:, :].rearrange("p (t e) -> p t e", e=E)[:, :, e].unsqueeze(2).broadcast_to([P, NT, n])
                dve.tensor_tensor(oh_cm[:, e], col(cm, CM), iota_cm[:, :].unsqueeze(1).broadcast_to([P, NT, CM]),
                                  ALU.is_equal)
                link(dve.tensor_tensor(oh_maj[:, e], col(maj, MAJ), iota_maj[:, :].unsqueeze(1).broadcast_to([P, NT, MAJ]),
                                       ALU.is_equal))
                dve.tensor_tensor(oh_tok[:, e], oh_maj[:, e], token_id[:, :].unsqueeze(2).broadcast_to([P, NT, MAJ]),
                                  ALU.mult).then_inc(onehot_ready, 1)

            def copy_grid(e):
                dve.wait_ge(grid_done, e + 1)
                dve.tensor_copy(grid[:, e, :], ps_grid[0:MAJ, 0:CM]).then_inc(grid_ready, 1)

            def copy_index(e):
                dve.wait_ge(index_done, e + 1)
                dve.tensor_copy(index[:, e, :], ps_grid[:, 64:64 + NC]).then_inc(index_ready, 1)

            def tokens_in(e):
                dve.wait_ge(xgT_done, e + 1)
                if e >= 2:
                    dve.wait_ge(h_done, HC * (e - 1))
                dve.tensor_copy(xgT[:, e % 2, :], ps_x[:, 0:CAP]).then_inc(xgT_ready, 1)

            def tokens_out(e):
                dve.wait_ge(y_done, e + 1)
                full = CAP // P
                last = CHUNKS[-1][1]
                dve.tensor_tensor(yb[:, e % 2, 0:full, :], ps_y[:, 0:full * C].rearrange("p (n c) -> p n c", c=C),
                                  b2_sb[:, e, :].unsqueeze(1).broadcast_to([P, full, C]), ALU.add)
                link(dve.tensor_tensor(yb[0:last, e % 2, full, :], ps_y[0:last, full * C:(full + 1) * C],
                                       b2_sb[0:last, e, :], ALU.add))
                dve.tensor_tensor(y[:, e, 0:full, :], yb[:, e % 2, 0:full, :],
                                  xg[:, e, 0:full, C + e:C + e + 1].broadcast_to([P, full, C]), ALU.mult)
                dve.tensor_scalar(y[0:last, e, full, :], yb[0:last, e % 2, full, :], xg[0:last, e, full, C + e:C + e + 1],
                                  None, ALU.mult).then_inc(y_ready, 1)

            dve.wait_ge(b_in, 32)
            onehots(0)
            for e in range(LEAD):
                copy_grid(e)
                onehots(e + 1)
                copy_index(e)
            tokens_in(0)
            for e in range(E):
                if e + 1 < E:
                    tokens_in(e + 1)
                if e + LEAD < E:
                    copy_grid(e + LEAD)
                    if e + LEAD + 1 < E:
                        onehots(e + LEAD + 1)
                    copy_index(e + LEAD)
                tokens_out(e)

        @block.tensor
        def _(pe):
            vr = vec_rows[:, :, :, :].rearrange("p k h d -> p k (h d)")

            def transpose_x(b):
                pe.wait_ge(x_in[b], 16)
                if b == 0:
                    pe.wait_ge(ident_ready, 1)
                else:
                    pe.wait_ge(T_copied, b)
                for i in range(TPB):
                    ins = pe.transpose(ps_T[:, i * P:(i + 1) * P], x_sb[:, b * TPB + i, :], ident[:, :])
                ins.then_inc(T_done, 1)

            def project(b):
                pe.wait_ge(T_copied, b + 1)
                if b == 0:
                    pe.wait_ge(wc_ready, 1)
                else:
                    pe.wait_ge(q_copied, 2 * b)
                pe.matmul(ps_q[:, 0:N], w_c[:, 0:C], xT[:, cols(b)], start=True, stop=True).then_inc(q_done, 1)
                if b >= 1:
                    pe.wait_ge(kv_copied, 4 * b)
                for i in range(TPB):
                    t = b * TPB + i
                    ins = pe.matmul(ps_kv[:, i * 2 * C:(i + 1) * 2 * C], xT[:, t * P:(t + 1) * P],
                                    w_c[:, C:3 * C], start=True, stop=True)
                ins.then_inc(kv_done, 1)

            def sum_q(b):
                pe.wait_ge(q_copied, 2 * b + 1)
                if b == 0:
                    pe.wait_ge(const_ready, 1)
                else:
                    pe.wait_ge(qvar_ready, b)
                for i in range(TPB):
                    t = b * TPB + i
                    ins = pe.matmul(ps_qss[:, i * HEADS:(i + 1) * HEADS], qsqT[:, t * P:(t + 1) * P],
                                    head_mask[:, ::DH], start=True, stop=True)
                ins.then_inc(qss_done, 1)

            def correlate(b):
                pe.wait_ge(kn_ready, b + 1)
                pe.wait_ge(kv_copied, 4 * (b + 1))
                if b >= 1:
                    pe.wait_ge(dots_ready, b)
                for i in range(TPB):
                    t = b * TPB + i
                    pe.matmul(ps_d[:, 0:P], vr[:, 3, :], kv[:, t, C:2 * C], start=(i == 0), stop=False)
                for i in range(TPB):
                    t = b * TPB + i
                    ins = pe.matmul(ps_d[:, 0:P], kn[:, t, :], kv[:, t, C:2 * C], start=False, stop=(i == TPB - 1))
                ins.then_inc(d_done, 1)

            def attend(b):
                pe.wait_ge(q_copied, 2 * (b + 1))
                pe.wait_ge(dots_ready, b + 1)
                if b >= 1:
                    pe.wait_ge(o_used, b)
                for i in range(TPB):
                    t = b * TPB + i
                    pe.matmul(ps_o[:, i * P:(i + 1) * P], qT[:, t * P:(t + 1) * P], dots_q[:, b, :],
                              start=True, stop=True)
                pe.matmul(ps_o[:, TPB * P:TPB * P + P], qbeta_mat[:, :], dots_b[:, b, :],
                          start=True, stop=True).then_inc(o_done, 1)

            def transpose_x1(b):
                pe.wait_ge(x1_ready, b + 1)
                if b >= 1:
                    pe.wait_ge(T1_copied, b)
                for i in range(TPB):
                    ins = pe.transpose(ps_T1[:, i * P:(i + 1) * P], x1[:, b * TPB + i, :], ident[:, :])
                ins.then_inc(T1_done, 1)

            def gate(b):
                pe.wait_ge(T1_copied, b + 1)
                for i in range(TPB):
                    t = b * TPB + i
                    ins = pe.matmul(ps_logit[:, t * E:(t + 1) * E], x1T[:, t * P:(t + 1) * P], gateT[:, :],
                                    start=True, stop=True)
                ins.then_inc(logit_done, 1)

            for s in range(STEPS):
                if live(s - 3):
                    attend(s - 3)
                if live(s):
                    transpose_x(s)
                if s == 0:
                    pe.wait_ge(wh_ready, 1)
                    pe.wait_ge(const_ready, 1)
                    pe.matmul(ps_T1[:, 0:3 * C], col_mean[:, :], w_h[:, :], start=True, stop=True).then_inc(wmean_done, 1)
                if live(s - 1):
                    sum_q(s - 1)
                if live(s - 2):
                    correlate(s - 2)
                if live(s):
                    project(s)
                if s == 0:
                    pe.wait_ge(vec_ready, 1)
                    pe.wait_ge(gatec_ready, 1)
                    pe.transpose(ps_small[:, 0:1], vr[0:1, 0, :], ident[0:1, 0:1])
                    pe.transpose(ps_small[:, 8:8 + E], gate_c[:, :], ident[0:E, 0:E])
                    pe.transpose(ps_small[:, 128:256], vr[:, 1, :], ident[:, :]).then_inc(small_T, 1)
                if live(s - 4):
                    transpose_x1(s - 4)
                if live(s - 5):
                    gate(s - 5)

            pe.wait_ge(b_in, 32)
            pe.transpose(ps_T[:, 0:E * HC], b1_rows[:, :], ident[0:E * HC, 0:E * HC]).then_inc(b1T_done, 1)
            pe.wait_ge(routed_ready, 1)
            pe.transpose(ps_small[:, 0:P], g3[:, :, :].rearrange("p t e -> p (t e)"), ident[:, :]).then_inc(wT_done, 1)
            pe.wait_ge(same_ready, 1)
            for r in range(ROUNDS):
                pe.wait_ge(counted, r + 1)
                pe.matmul(ps_cnt[:, 0:CAND], same_e[:, :], count[:, r % 2, :], start=True, stop=True).then_inc(summed, 1)
            pe.wait_ge(counted, ROUNDS + 1)
            pe.wait_ge(before_ready, 1)
            pe.matmul(ps_cnt[:, 0:2], same_e[:, :], cnt2[:, :], start=True, stop=True)
            pe.matmul(ps_cnt[:, 2:4], before_e[:, :], cnt2[:, :], start=True, stop=True).then_inc(summed, 1)
            pe.wait_ge(pos_ready, 1)
            pe.transpose(ps_small[:, P:2 * P], pos[:, :], ident[:, :]).then_inc(slotT_done, 1)

            def find_tokens(e):
                pe.wait_ge(onehot_ready, e + 1)
                if e >= 1:
                    pe.wait_ge(index_ready, e)
                for t in range(NT):
                    ins = pe.matmul(ps_grid[0:MAJ, 0:CM], oh_tok[:, e, t, :], oh_cm[:, e, t, :],
                                    start=(t == 0), stop=(t == NT - 1))
                ins.then_inc(grid_done, 1)

            def spread_tokens(e):
                pe.wait_ge(grid_ready, e + 1)
                for b in range(SUB):
                    ins = pe.matmul(ps_grid[:, 64:64 + NC], spread[:, b, :],
                                    grid[:, e, :].rearrange("a (c b) -> a c b", b=SUB)[:, :, b],
                                    start=(b == 0), stop=(b == SUB - 1))
                ins.then_inc(index_done, 1)

            def tokens_in(e):
                pe.wait_ge(gathered[e], 16 * NC)
                if e >= 1:
                    pe.wait_ge(xgT_ready, e)
                for c, (at, n) in enumerate(CHUNKS):
                    ins = pe.transpose(ps_x[:, at:at + n], xg[0:n, e, c, 0:C], ident[0:n, 0:n])
                ins.then_inc(xgT_done, 1)

            def up(e):
                pe.wait_ge(xgT_ready, e + 1)
                for c in range(HC):
                    if e >= 1:
                        pe.wait_ge(h_ready, HC * (e - 1) + c + 1)
                    pe.matmul(ps_h[c][:, 0:CAP], w1_sb[:, e, c * P:(c + 1) * P], xgT[:, e % 2, :],
                              start=True, stop=True).then_inc(h_done, 1)

            def down(e):
                pe.wait_ge(h_ready, HC * (e + 1))
                if e >= 1:
                    pe.wait_ge(y_ready, e)
                for k, (at, n) in enumerate(CHUNKS):
                    for c in range(HC):
                        ins = pe.matmul(ps_y[0:n, k * C:(k + 1) * C], hid[:, e % 2, c, at:at + n], w2_sb[:, e, c, :],
                                        start=(c == 0), stop=(c == HC - 1))
                ins.then_inc(y_done, 1)

            for e in range(LEAD):
                find_tokens(e)
                spread_tokens(e)
            pe.wait_ge(w1_in, 16)
            pe.wait_ge(w2_in, 16)
            tokens_in(0)
            up(0)
            for e in range(E):
                if e + 1 < E:
                    tokens_in(e + 1)
                if e + LEAD < E:
                    find_tokens(e + LEAD)
                if e + 1 < E:
                    up(e + 1)
                if e + LEAD < E:
                    spread_tokens(e + LEAD)
                down(e)


_INS = ['x', 'L0_conv_w_qkv', 'L0_conv_q_gamma', 'L0_conv_q_beta', 'L0_conv_k_gamma', 'L0_conv_k_beta',
        'L0_ffn_gate_w', 'L0_ffn_gate_b', 'L0_ffn_w1', 'L0_ffn_b1', 'L0_ffn_w2', 'L0_ffn_b2']


def kernel(**inputs):
    import numpy as _np
    import concourse.bacc as _bacc
    from concourse import mybir as _mybir
    from concourse.bass_utils import run_bass_kernel_spmd as _run

    nc = _bacc.Bacc("TRN2", target_bir_lowering=False, num_devices=1)
    arrays, args = {}, []
    for name in _INS:
        a = _np.ascontiguousarray(inputs[name])
        arrays[f"in_{name}_dram"] = a
        args.append(nc.dram_tensor(f"in_{name}_dram", a.shape, _mybir.dt.from_np(a.dtype), kind="ExternalInput").ap())
    shape = inputs['x'].shape
    out = nc.dram_tensor("out_0_dram", shape, _mybir.dt.float32, kind="ExternalOutput").ap()
    build(nc, *args, out)
    r = _run(nc, [arrays], core_ids=[0])
    return r.results[0]["out_0_dram"]
```

```python
from contextlib import ExitStack

import numpy as np

import concourse.bass as bass
from concourse import mybir

F32 = mybir.dt.float32
F16 = mybir.dt.float16
BF16 = mybir.dt.bfloat16
I32 = mybir.dt.int32
U16 = mybir.dt.uint16
U32 = mybir.dt.uint32
ALU = mybir.AluOpType
ACT = mybir.ActivationFunctionType
AX = mybir.AxisListType.X

P = 128
HEADS, DH = 8, 16
TOPK = 2
CAP_FACTOR = 1.2
LN_C_EPS, LN_H_EPS, LN_T_EPS = 1e-6, 1e-5, 1e-5
UPPER_DIGITS = (4, 4, 3, 3)
LOWER_DIGITS = (3, 3, 3, 3, 4)


def build(nc, x, w_qkv, q_gamma, q_beta, k_gamma, k_beta, gate_w, gate_b, w1, b1, w2, b2, out):
    B, L, W, C = x.shape
    N = L * W
    T = B * N
    E, _, HID = w1.shape
    NT = T // P
    TPB = N // P
    HC = HID // P
    CAP = int(CAP_FACTOR * T / E)
    CHUNKS = [(c * P, min(P, CAP - c * P)) for c in range(-(-CAP // P))]
    NC = len(CHUNKS)
    LAST, HALF = NC - 1, P // 2
    assert CHUNKS[LAST][1] <= HALF and E % 2 == 0
    TE = NT * E
    ROW = C + E
    MAJ = 16
    SUB = P // MAJ
    CM = NC * SUB
    ROUNDS = [(half, sum(ds[i + 1:]), d) for half, ds in enumerate((UPPER_DIGITS, LOWER_DIGITS)) for i, d in enumerate(ds)]
    NR = len(ROUNDS)
    CAND = 2 ** max(d for _, _, d in ROUNDS) - 1
    CUTS = (0, 3 * NT // 8, 3 * NT // 4, NT)
    GATHERS_AFTER = (13, 1, 2, 2, 1, 1)
    X_PARTS = [(0, 1), (1, 2), (2, B // 2), (B // 2, B)]

    def part_of(b):
        return next(n for n, (_, end) in enumerate(X_PARTS) if b < end)

    assert C == P and TE == P and HEADS * DH == C

    x_d = x.rearrange("b l w c -> (b l w) c").rearrange("(t p) c -> p t c", p=P)
    out_rows = out.rearrange("b l w c -> (b l w) c")
    out_d = out_rows.rearrange("(t p) c -> p t c", p=P)
    table = nc.dram_tensor("table", [T, ROW], F32, kind="Internal").ap()
    table_d = table.rearrange("(t p) c -> p t c", p=P)

    with ExitStack() as ctx:
        def sb(name, shape, dt=F32):
            return ctx.enter_context(nc.sbuf_tensor(name, shape, dt))

        def sem(name):
            return ctx.enter_context(nc.semaphore(name))

        x_sb = sb("x_sb", [P, NT, C])
        wqkv = sb("wqkv", [C, 3 * C])
        vecs = sb("vecs", [P, 4, DH])
        gate_rows = sb("gate_rows", [E, C])
        gate_bias = sb("gate_bias", [P, E])
        b1_rows = sb("b1_rows", [E * HC, P])
        b2_sb = sb("b2_sb", [P, E, C])
        w1_sb = sb("w1_sb", [C, E, HID])
        w2_sb = sb("w2_sb", [P, E, HC, C])
        ident = sb("ident", [P, P])
        ones = sb("ones", [P, P])
        head_mask = sb("head_mask", [P, P])
        sqrt_first = sb("sqrt_first", [P, 1])
        head_mean = sb("head_mean", [P, P])
        upto = sb("upto", [P, P], BF16)
        warm_rhs = sb("warm_rhs", [P, 512], BF16)
        ones16 = sb("ones16", [P, P], BF16)
        token_id = sb("token_id", [P, NT])
        iota_maj = sb("iota_maj", [P, MAJ])
        iota_cm = sb("iota_cm", [P, CM])
        digits = sb("digits", [P, CAND, E])
        tile_run = sb("tile_run", [P, 2, E, NT])
        expert_run = sb("expert_run", [P, TE])
        spread = sb("spread", [MAJ, SUB, P], F16)
        eps = sb("eps", [P, 2])
        zero1 = sb("zero1", [P, 1])
        col_mean = sb("col_mean", [P, P])
        w_h = sb("w_h", [C, 3 * C])
        w_c = sb("w_c", [C, 3 * C])
        w_sum = sb("w_sum", [C, 2 * HEADS])
        q_rows = sb("q_rows", [1, 2, HEADS, DH])
        q_cols = sb("q_cols", [P, 2])
        kbeta_rows = sb("kbeta_rows", [P, HEADS, DH])
        stat = sb("stat", [P, NT, 6])
        mv = sb("mv", [P, NT, 2])
        eps_var = sb("eps_var", [P, NT])
        std = sb("std", [P, NT])
        rstd = sb("rstd", [P, NT])
        xT = sb("xT", [C, T])
        q_work = sb("q_work", [P, 2, T])
        qT, qsqT = q_work[:, 0, :], q_work[:, 1, :]
        kv = sb("kv", [P, NT, 2 * C])
        ksq = sb("ksq", [P, NT, C])
        kss = sb("kss", [P, NT, HEADS])
        kq_var = sb("kq_var", [P, NT, 2, HEADS])
        kq_std = sb("kq_std", [P, NT, 2, HEADS])
        kq_rstd = sb("kq_rstd", [P, NT, 2, HEADS])
        kn = ksq
        dots = sb("dots", [P, B, P])
        att = sb("att", [P, NT, C])
        xb = sb("xb", [P, NT, C])
        x1 = att
        stat2 = sb("stat2", [P, NT, 6])
        mv2 = sb("mv2", [P, NT, 2])
        std2 = sb("std2", [P, NT])
        rstd2 = sb("rstd2", [P, NT])
        rows = sb("rows", [P, NT, ROW])
        x1T = xT
        shift2 = sb("shift2", [P, NT])
        gate_c = sb("gate_c", [E, C])
        gate_sum = sb("gate_sum", [E, 1])
        gateT = sb("gateT", [C, E])
        b1T = sb("b1T", [P, E * HC])
        logit = sb("logit", [P, NT, E])
        shifted = sb("shifted", [P, NT, E])
        expd = sb("expd", [P, NT, E])
        prob = sb("prob", [P, NT, E])
        g1 = sb("g1", [P, NT, E])
        g2 = sb("g2", [P, NT, E])
        g3 = sb("g3", [P, NT, E])
        g4 = sb("g4", [P, NT, E])
        s1 = sb("s1", [P, NT])
        s2 = sb("s2", [P, NT])
        s3 = sb("s3", [P, NT])
        s4 = sb("s4", [P, NT])
        s5 = sb("s5", [P, NT])
        upper = sb("upper", [P, NT, E], U16)
        lower = sb("lower", [P, NT, E], U16)
        below_all = sb("below_all", [P, NT, E], U16)
        same_upper = sb("same_upper", [P, NT, E], U16)
        keys = sb("keys", [P, NT, E], U16)
        cand = sb("cand", [P, 2, CAND, E], U16)
        hits = sb("hits", [P, 2, CAND, NT, E], BF16)
        best = sb("best", [P, NR + 2, CAND + 1, E])
        thr_upper = sb("thr_upper", [P, E], I32)
        thr_lower = sb("thr_lower", [P, E], I32)
        thr = sb("thr", [P, E], I32)
        member = sb("member", [P, 2, E, NT], BF16)
        members = sb("members", [P, 2, E, NT], BF16)
        need = sb("need", [P, E])
        fits = sb("fits", [P, E, NT])
        capped = sb("capped", [P, E, NT])
        taken = sb("taken", [P, E, NT])
        pos = sb("pos", [P, E, NT])
        slot = sb("slot", [P, TE], I32)
        maj = sb("maj", [P, TE], I32)
        cm = sb("cm", [P, TE], I32)
        oh_maj = sb("oh_maj", [P, E, NT, MAJ], F16)
        oh_tok = sb("oh_tok", [P, E, NT, MAJ], F16)
        oh_cm = sb("oh_cm", [P, E, NT, CM], F16)
        grid = sb("grid", [MAJ, E, CM], F16)
        index = sb("index", [P, E, NC + 1], U32)
        PAIR_ROWS = 2 * LAST + 1
        xg = kv[:, :, :].rearrange("p t c -> p (t c)")[:, 0:E // 2 * PAIR_ROWS * ROW].rearrange(
            "p (g n r) -> p g n r", g=E // 2, n=PAIR_ROWS)
        gelu_first = sb("gelu_first", [P, 1])
        xgT = sb("xgT", [C, 2, CAP])
        hid = sb("hid", [P, 2, HC, CAP])
        wb2 = sb("wb2", [P, 2, NC, C])
        y = q_work[:, :, :].rearrange("p a t -> p (a t)")[:, 0:E * NC * C].rearrange(
            "p (e n c) -> p e n c", e=E, n=NC)

        banks = [ctx.enter_context(nc.psum_tensor(f"bank{i}", [P, 512], F32)) for i in range(8)]
        ps_T, ps_q, ps_kv, ps_d, ps_o, ps_T1, ps_qss, misc = banks
        ps_logit = misc[:, 0:TE]
        ps_small = misc[:, 256:512]
        ps_run = banks[1][:, 0:2 * TE]
        ps_total = banks[1][:, 2 * TE:2 * TE + E]
        ps_h = [banks[1], banks[2], banks[3], banks[4]]
        ps_x = banks[0]
        ps_ys = [banks[5], banks[7]]
        ps_grid = banks[6]
        ps_cnt = banks[7]

        x_in = [sem(f"x_in{n}") for n in range(len(X_PARTS))]
        wqkv_in, vecs_in, gate_in, b_in, w1_in, w2_in = (sem(n) for n in (
            "wqkv_in", "vecs_in", "gate_in", "b_in", "w1_in", "w2_in"))
        pool_step, dve_step = sem("pool_step"), sem("dve_step")
        ident_ready, const_ready, warm_ready = sem("ident_ready"), sem("const_ready"), sem("warm_ready")
        wh_ready, wv_ready, wmean_done, wc_ready, vec_ready, gatec_ready = (
            sem("wh_ready"), sem("wv_ready"), sem("wmean_done"), sem("wc_ready"), sem("vec_ready"), sem("gatec_ready"))
        rows_ready = sem("rows_ready")
        cols_T, cols_ready, eps_ready = sem("cols_T"), sem("cols_ready"), sem("eps_ready")
        gate_T, b1T_done = sem("gate_T"), sem("b1T_done")
        var_ready, std_ready, rstd_ready = sem("var_ready"), sem("std_ready"), sem("rstd_ready")
        T_done, T_copied = sem("T_done"), sem("T_copied")
        q_done, q_copied, kv_done, kv_copied = sem("q_done"), sem("q_copied"), sem("kv_done"), sem("kv_copied")
        qss_done, kqvar_ready, kqstd_ready, kqrstd_ready, kn_ready = (
            sem("qss_done"), sem("kqvar_ready"), sem("kqstd_ready"), sem("kqrstd_ready"), sem("kn_ready"))
        d_done, dots_ready, o_done, o_used, x1_ready = (
            sem("d_done"), sem("dots_ready"), sem("o_done"), sem("o_used"), sem("x1_ready"))
        var2_ready, std2_ready, shift2_ready, x2_ready = (
            sem("var2_ready"), sem("std2_ready"), sem("shift2_ready"), sem("x2_ready"))
        T1_done, T1_copied, logit_done = sem("T1_done"), sem("T1_copied"), sem("logit_done")
        shifted_ready, exp_ready, routed_ready = sem("shifted_ready"), sem("exp_ready"), sem("routed_ready")
        compared, summed, member_ready, run_done = (
            sem("compared"), sem("summed"), sem("member_ready"), sem("run_done"))
        onehot_ready, grid_done, grid_ready, index_done, index_ready = (
            sem("onehot_ready"), sem("grid_done"), sem("grid_ready"), sem("index_done"), sem("index_ready"))
        pair_gathered = [sem(f"pair_gathered{g}") for g in range(E // 2)]
        gathered = [sem(f"gathered{e}") for e in range(E)]
        xgT_done, xgT_ready, h_done, h_ready, y_done, y_ready = (
            sem("xgT_done"), sem("xgT_ready"), sem("h_done"), sem("h_ready"), sem("y_done"), sem("y_ready"))
        table_out, out_init = sem("table_out"), sem("out_init")
        added = [sem(f"added{e}") for e in range(E)]

        block = ctx.enter_context(nc.Block())

        def img(b):
            return slice(b * TPB, (b + 1) * TPB)

        def cols(b):
            return slice(b * N, (b + 1) * N)

        def xg_chunk(e, c):
            if c < LAST:
                return xg[:, e // 2, e % 2 * LAST + c, :]
            at = e % 2 * HALF
            return xg[at:at + CHUNKS[LAST][1], e // 2, 2 * LAST, :]

        STEPS = B + 5

        def live(b):
            return 0 <= b < B

        @block.sync
        def _(sp):
            for n, (b0, b1_) in enumerate(X_PARTS):
                part = slice(b0 * TPB, b1_ * TPB)
                sp.dma_start(x_sb[:, part, :], x_d[:, part, :]).then_inc(x_in[n], 16)
                if n == 0:
                    sp.dma_start(wqkv[:, :], w_qkv).then_inc(wqkv_in, 16)
                if n == 1:
                    for k, v in enumerate((q_gamma, q_beta, k_gamma, k_beta)):
                        sp.dma_start(vecs[:, k, :], v.partition_broadcast(P)).then_inc(vecs_in, 16)
                    sp.dma_start(gate_rows[:, :], gate_w).then_inc(gate_in, 16)
            sp.dma_start(gate_bias[:, :], gate_b.partition_broadcast(P)).then_inc(gate_in, 16)
            sp.dma_start(b1_rows[:, :], b1.rearrange("e (c p) -> (e c) p", p=P)).then_inc(b_in, 16)
            sp.dma_start(w1_sb[:, :, :], w1.rearrange("e c h -> c e h")).then_inc(w1_in, 16)
            sp.dma_start(w2_sb[:, :, :, :].rearrange("p e c d -> p (e c) d"),
                         w2.rearrange("e (c p) d -> p (e c) d", p=P)).then_inc(w2_in, 16)
            sp.dma_start(b2_sb[:, :, :].rearrange("p e c -> p (e c)"),
                         b2.rearrange("e c -> (e c)").partition_broadcast(P)).then_inc(b_in, 16)
            for b in range(B):
                sp.wait_ge(x1_ready, b + 1)
                sp.dma_start(out_d[:, img(b), :], x1[:, img(b), :]).then_inc(out_init, 16)
            sp.wait_ge(x2_ready, NT)
            sp.wait_ge(routed_ready, 1)
            sp.dma_start(table_d, rows[:, :, :]).then_inc(table_out, 16)
            sp.wait_ge(out_init, 16 * B)
            sp.wait_ge(table_out, 16)
            for e in range(E):
                sp.wait_ge(added[e], 16 * NC)

        @block.gpsimd
        def _(pool):
            steps = [0]

            def link(ins):
                steps[0] += 1
                ins.then_inc(pool_step, 1)
                pool.wait_ge(pool_step, steps[0])

            pool.memset(eps[:, 0:1], LN_C_EPS)
            pool.memset(eps[:, 1:2], LN_H_EPS).then_inc(eps_ready, 1)
            pool.memset(warm_rhs[:, :], 0.0).then_inc(warm_ready, 1)
            link(pool.memset(ident[:, :], 0.0))
            pool.affine_select(out=ident[:, :], in_=ident[:, :], compare_op=ALU.not_equal, fill=1.0,
                               base=0, pattern=[[-1, P]], channel_multiplier=1).then_inc(ident_ready, 1)
            pool.memset(col_mean[:, :], 1.0 / C)
            link(pool.memset(ones[:, :], 1.0))
            hm = head_mask[:, :].rearrange("p (h d) -> p h d", d=DH)
            link(pool.affine_select(out=hm, in_=ones[:, :].rearrange("p (h d) -> p h d", d=DH),
                                    compare_op=ALU.is_ge, fill=0.0, base=0,
                                    pattern=[[-DH, HEADS], [0, DH]], channel_multiplier=1))
            link(pool.affine_select(out=hm, in_=hm, compare_op=ALU.is_ge, fill=0.0, base=DH - 1,
                                    pattern=[[DH, HEADS], [0, DH]], channel_multiplier=-1))
            pool.tensor_scalar(head_mean[:, :], head_mask[:, :], 1.0 / N, None, ALU.mult).then_inc(const_ready, 1)

            def late_constants():
                link(pool.memset(upto[:, :], 0.0))
                pool.affine_select(out=upto[:, :], in_=upto[:, :], compare_op=ALU.is_ge, fill=-1.0,
                                   base=0, pattern=[[1, P]], channel_multiplier=-1)
                pool.memset(ones16[:, :], 1.0)
                pool.memset(tile_run[:, :, :, :], 1.0)
                pool.memset(best[:, :, 0, :], 0.0)
                pool.memset(expert_run[:, :], 1.0)
                pool.iota(digits[:, :, :], [[1, CAND], [0, E]], base=1, channel_multiplier=0, allow_small_or_imprecise_dtypes=True)
                pool.iota(token_id[:, :], [[P, NT]], base=0, channel_multiplier=1, allow_small_or_imprecise_dtypes=True)
                pool.iota(iota_maj[:, :], [[1, MAJ]], base=0, channel_multiplier=0, allow_small_or_imprecise_dtypes=True)
                pool.iota(iota_cm[:, :], [[1, CM]], base=0, channel_multiplier=0, allow_small_or_imprecise_dtypes=True)
                link(pool.memset(spread[:, :, :], 0.0))
                pool.memset(tile_run[:, :, :, 0:1], 0.0)
                pool.memset(expert_run[:, :].rearrange("p (t e) -> p t e", e=E)[:, :, 0:1], 0.0)
                pool.affine_select(out=spread[:, :, :], in_=spread[:, :, :], compare_op=ALU.not_equal, fill=1.0,
                                   base=0, pattern=[[-MAJ, SUB], [1, P]], channel_multiplier=-1).then_inc(const_ready, 1)

            def scale_k(b):
                def by_head(a):
                    return a.rearrange("p t (h d) -> p t h d", d=DH)
                pool.wait_ge(kv_copied, 4 * b + 2)
                pool.wait_ge(kqrstd_ready, b + 1)
                link(pool.tensor_tensor(by_head(kn[:, img(b), :]), by_head(kv[:, img(b), 0:C]),
                                        kq_rstd[:, img(b), 0, :].unsqueeze(3).broadcast_to([P, TPB, HEADS, DH]), ALU.mult))
                pool.tensor_tensor(by_head(kn[:, img(b), :]), by_head(kn[:, img(b), :]),
                                   vecs[:, 2, :].unsqueeze(1).unsqueeze(1).broadcast_to([P, TPB, HEADS, DH]),
                                   ALU.mult).then_inc(kn_ready, 1)

            def residual(b):
                pool.wait_ge(o_used, b + 1)
                pool.tensor_tensor(x1[:, img(b), :], att[:, img(b), :], xb[:, img(b), :], ALU.add).then_inc(x1_ready, 1)

            pool.wait_ge(vecs_in, 64)
            pool.tensor_copy(kbeta_rows[:, :, :],
                             vecs[:, 3, :].unsqueeze(1).broadcast_to([P, HEADS, DH])).then_inc(vec_ready, 1)
            for s in range(STEPS):
                if live(s - 3):
                    residual(s - 3)
                if live(s - 1):
                    scale_k(s - 1)
            late_constants()

            def gather(e, c):
                pool.wait_ge(index_ready, e + 1)
                if c < LAST:
                    pool.indirect_dma_start(
                        out=xg_chunk(e, c), out_offset=None, in_=table,
                        in_offset=bass.IndirectOffsetOnAxis(ap=index[:, e, c:c + 1], axis=0)).then_inc(gathered[e], 16)
                else:
                    n = HALF + CHUNKS[LAST][1]
                    pool.indirect_dma_start(
                        out=xg[0:n, e // 2, 2 * LAST, :], out_offset=None, in_=table,
                        in_offset=bass.IndirectOffsetOnAxis(ap=index[0:n, e, NC:NC + 1], axis=0)
                    ).then_inc(pair_gathered[e // 2], 16)

            def scatter(e):
                if e == 0:
                    pool.wait_ge(out_init, 16 * B)
                else:
                    pool.wait_ge(added[e - 1], 16 * NC)
                for c, (_, n) in enumerate(CHUNKS):
                    pool.wait_ge(y_ready, NC * e + c + 1)
                    pool.indirect_dma_start(
                        out=out_rows, out_offset=bass.IndirectOffsetOnAxis(ap=index[0:n, e, c:c + 1], axis=0),
                        in_=y[0:n, e, c, :], in_offset=None, compute_op=ALU.add).then_inc(added[e], 16)

            pool.wait_ge(table_out, 16)
            order = []
            for e in range(0, E, 2):
                order += [(e, c) for c in range(LAST)] + [(e + 1, LAST)] + [(e + 1, c) for c in range(LAST)]
            assert sum(GATHERS_AFTER) == len(order)
            done = 0
            for e in range(-1, E):
                if e >= 0:
                    scatter(e)
                n = GATHERS_AFTER[e + 1] if e + 1 < len(GATHERS_AFTER) else 0
                for next_e, c in order[done:done + n]:
                    gather(next_e, c)
                done += n

        @block.scalar
        def _(act):
            def copy_xT(b):
                act.wait_ge(T_done, b + 1)
                act.activation(xT[:, cols(b)], ps_T[:, 0:N], ACT.Copy).then_inc(T_copied, 1)

            def token_std(b):
                act.wait_ge(var_ready, b + 1)
                act.activation(std[:, img(b)], mv[:, img(b), 1], ACT.Sqrt, bias=eps[:, 0:1]).then_inc(std_ready, 1)

            act.wait_ge(eps_ready, 1)
            act.activation(sqrt_first[:, :], eps[:, 0:1], ACT.Sqrt)
            act.wait_ge(wqkv_in, 16)
            act.activation(w_h[:, 2 * C:3 * C], wqkv[:, 2 * C:3 * C], ACT.Copy).then_inc(wv_ready, 1)
            copy_xT(0)
            token_std(0)
            act.wait_ge(vecs_in, 64)
            act.activation(q_rows[:, :, :, :], vecs[0:1, 0:2, :].unsqueeze(2).broadcast_to([1, 2, HEADS, DH]),
                           ACT.Copy).then_inc(rows_ready, 1)
            act.wait_ge(cols_T, 1)
            act.activation(q_cols[:, :], ps_small[:, 0:2], ACT.Copy).then_inc(cols_ready, 1)
            act.wait_ge(cols_ready, 1)
            for s in range(STEPS):
                if live(s + 1):
                    copy_xT(s + 1)
                if live(s + 1):
                    token_std(s + 1)
                if live(s):
                    act.wait_ge(q_done, s + 1)
                    act.activation(qsqT[:, cols(s)], ps_q[:, 0:N], ACT.Square).then_inc(q_copied, 1)
                    act.activation(qT[:, cols(s)], ps_q[:, 0:N], ACT.Copy, scale=q_cols[:, 0:1]).then_inc(q_copied, 1)
                if live(s - 1):
                    act.wait_ge(kqvar_ready, s)
                    act.activation(kq_std[:, img(s - 1), :, :], kq_var[:, img(s - 1), :, :], ACT.Sqrt,
                                   bias=zero1[:, :]).then_inc(kqstd_ready, 1)
                if live(s):
                    src = ps_kv[:, :].rearrange("p (t c) -> p t c", t=TPB)
                    act.wait_ge(kv_done, s + 1)
                    act.activation(ksq[:, img(s), :], src[:, :, 0:C], ACT.Square).then_inc(kv_copied, 1)
                    act.activation(kv[:, img(s), 0:C], src[:, :, 0:C], ACT.Copy).then_inc(kv_copied, 1)
                    act.wait_ge(rstd_ready, s + 1)
                    for i in range(TPB):
                        t = s * TPB + i
                        act.activation(kv[:, t, C:2 * C], src[:, i, C:2 * C], ACT.Copy,
                                       scale=rstd[:, t:t + 1]).then_inc(kv_copied, 1)
                if live(s - 4):
                    act.wait_ge(T1_done, s - 3)
                    act.activation(x1T[:, cols(s - 4)], ps_T1[:, 0:N], ACT.Copy).then_inc(T1_copied, 1)

            act.wait_ge(var2_ready, 1)
            act.activation(std2[:, :], mv2[:, :, 1], ACT.Sqrt, bias=eps[:, 1:2]).then_inc(std2_ready, 1)
            act.wait_ge(shifted_ready, 1)
            act.activation(expd[:, :, :], shifted[:, :, :], ACT.Exp).then_inc(exp_ready, 1)
            act.wait_ge(shift2_ready, 1)
            for t in range(NT):
                act.activation(rows[:, t, 0:C], x1[:, t, :], ACT.Identity, bias=shift2[:, t:t + 1],
                               scale=rstd2[:, t:t + 1]).then_inc(x2_ready, 1)

            def tokens_in(e):
                act.wait_ge(xgT_done, e + 1)
                act.activation(xgT[:, e % 2, :], ps_x[:, 0:CAP], ACT.Copy).then_inc(xgT_ready, 1)

            act.activation(gelu_first[:, :], eps[:, 0:1], ACT.Gelu)
            tokens_in(0)
            for e in range(E):
                if e == 1:
                    tokens_in(1)
                for c in range(HC):
                    act.wait_ge(h_done, HC * e + c + 1)
                    if e >= 2 and c == 0:
                        act.wait_ge(y_done, NC * (e - 1))
                    act.activation(hid[:, e % 2, c, :], ps_h[c][:, 0:CAP], ACT.Gelu,
                                   bias=b1T[:, e * HC + c:e * HC + c + 1]).then_inc(h_ready, 1)

        @block.vector
        def _(dve):
            steps = [0]

            def link(ins):
                steps[0] += 1
                ins.then_inc(dve_step, 1)
                dve.wait_ge(dve_step, steps[0])

            def stats(b):
                dve.wait_ge(x_in[part_of(b)], 16)
                for t in range(b * TPB, (b + 1) * TPB):
                    ins = dve.bn_stats(stat[:, t, :], x_sb[:, t, :])
                link(ins)
                for t in range(b * TPB, (b + 1) * TPB):
                    ins = dve.bn_aggr(mv[:, t, :], stat[:, t, :])
                ins.then_inc(var_ready, 1)

            def stats_rest(b):
                dve.wait_ge(var_ready, b + 1)
                dve.tensor_scalar(eps_var[:, img(b)], mv[:, img(b), 1], LN_C_EPS, LN_H_EPS, ALU.add, ALU.mult)
                dve.wait_ge(std_ready, b + 1)
                dve.reciprocal(rstd[:, img(b)], std[:, img(b)]).then_inc(rstd_ready, 1)

            stats(0)
            dve.wait_ge(wqkv_in, 16)
            wv = wqkv[:, 0:2 * C].rearrange("p (h d) -> p h d", d=DH)
            link(dve.tensor_reduce(w_sum[:, :], wv, AX, ALU.add))
            dve.scalar_tensor_tensor(w_h[:, 0:2 * C].rearrange("p (h d) -> p h d", d=DH),
                                     w_sum[:, :].unsqueeze(2).broadcast_to([C, 2 * HEADS, DH]), -1.0 / DH, wv,
                                     ALU.mult, ALU.add).then_inc(wh_ready, 1)
            dve.memset(zero1[:, :], 0.0)
            stats_rest(0)
            stats(1)
            dve.wait_ge(wmean_done, 1)
            dve.tensor_tensor(w_c[:, :], w_h[:, :], ps_T1[:, 0:3 * C], ALU.subtract).then_inc(wc_ready, 1)
            for b in range(2, 4):
                stats(b)
            stats_rest(1)

            for s in range(STEPS):
                if live(s - 1):
                    b = s - 1
                    token_part = eps_var[:, img(b)].unsqueeze(2).broadcast_to([P, TPB, HEADS])
                    dve.wait_ge(kv_copied, 4 * b + 1)
                    link(dve.tensor_reduce(kss[:, img(b), :], ksq[:, img(b), :].rearrange("p t (h d) -> p t h d", d=DH),
                                           AX, ALU.add))
                    dve.scalar_tensor_tensor(kq_var[:, img(b), 0, :], kss[:, img(b), :], 1.0 / DH, token_part,
                                             ALU.mult, ALU.add)
                    dve.wait_ge(qss_done, b + 1)
                    dve.scalar_tensor_tensor(kq_var[:, img(b), 1, :],
                                             ps_qss[:, 0:TPB * HEADS].rearrange("p (t h) -> p t h", h=HEADS), 1.0 / DH,
                                             token_part, ALU.mult, ALU.add).then_inc(kqvar_ready, 1)
                if s == 1:
                    dve.wait_ge(gate_in, 32)
                    link(dve.tensor_reduce(gate_sum[:, :], gate_rows[:, :], AX, ALU.add))
                    dve.scalar_tensor_tensor(gate_c[:, :], gate_sum[:, :].broadcast_to([E, C]), -1.0 / C, gate_rows[:, :],
                                             ALU.mult, ALU.add).then_inc(gatec_ready, 1)
                if s == 3:
                    dve.wait_ge(gate_T, 1)
                    dve.tensor_copy(gateT[:, :], ps_small[:, 8:8 + E])
                if live(s - 3):
                    b = s - 3
                    dve.wait_ge(kqrstd_ready, b + 1)
                    dve.wait_ge(o_done, b + 1)
                    dve.tensor_tensor(att[:, img(b), :].rearrange("p t (h d) -> p t h d", d=DH),
                                      ps_o[:, 0:TPB * P].rearrange("p (t h d) -> p t h d", h=HEADS, d=DH),
                                      kq_rstd[:, img(b), 1, :].unsqueeze(3).broadcast_to([P, TPB, HEADS, DH]), ALU.mult)
                    dve.tensor_tensor(xb[:, img(b), :], x_sb[:, img(b), :],
                                      ps_o[:, TPB * P:TPB * P + P].unsqueeze(1).broadcast_to([P, TPB, P]),
                                      ALU.add).then_inc(o_used, 1)
                if live(s - 1):
                    dve.wait_ge(kqstd_ready, s)
                    dve.reciprocal(kq_rstd[:, img(s - 1), :, :], kq_std[:, img(s - 1), :, :]).then_inc(kqrstd_ready, 1)
                if live(s - 2):
                    b = s - 2
                    dve.wait_ge(d_done, b + 1)
                    dve.tensor_tensor(dots[:, b, :], ps_d[:, 0:P], head_mean[:, :], ALU.mult).then_inc(dots_ready, 1)
                if live(s + 3) and s >= 1:
                    stats(s + 3)
                if live(s - 4):
                    b = s - 4
                    dve.wait_ge(x1_ready, b + 1)
                    for i in range(TPB):
                        ins = dve.bn_stats(stat2[:, b * TPB + i, :], x1[:, b * TPB + i, :])
                    link(ins)
                    for i in range(TPB):
                        ins = dve.bn_aggr(mv2[:, b * TPB + i, :], stat2[:, b * TPB + i, :])
                    if b == B - 1:
                        ins.then_inc(var2_ready, 1)
                if live(s + 1) and s >= 1:
                    stats_rest(s + 1)

            dve.wait_ge(std2_ready, 1)
            link(dve.reciprocal(rstd2[:, :], std2[:, :]))

            def per_tile(s):
                return s[:, :].unsqueeze(2).broadcast_to([P, NT, E])

            dve.wait_ge(logit_done, B)
            link(dve.tensor_tensor(logit[:, :, :], ps_logit.rearrange("p (t e) -> p t e", e=E), per_tile(rstd2), ALU.mult))
            link(dve.tensor_tensor(logit[:, :, :], logit[:, :, :],
                                   gate_bias[:, :].unsqueeze(1).broadcast_to([P, NT, E]), ALU.add))
            link(dve.tensor_reduce(s1[:, :], logit[:, :, :], AX, ALU.max))
            dve.tensor_tensor(shifted[:, :, :], logit[:, :, :], per_tile(s1), ALU.subtract).then_inc(shifted_ready, 1)
            dve.scalar_tensor_tensor(shift2[:, :], mv2[:, :, 0], -1.0, rstd2[:, :], ALU.mult, ALU.mult).then_inc(shift2_ready, 1)
            dve.wait_ge(exp_ready, 1)
            dve.scalar_tensor_tensor(g1[:, :, :], expd[:, :, :], 1.0, expd[:, :, :], ALU.is_lt, ALU.mult)
            link(dve.tensor_scalar(g2[:, :, :], expd[:, :, :], 1.0, None, ALU.is_ge))
            dve.tensor_reduce(s2[:, :], g1[:, :, :], AX, ALU.max)
            link(dve.tensor_reduce(s3[:, :], g2[:, :, :], AX, ALU.add))
            link(dve.scalar_tensor_tensor(s4[:, :], s3[:, :], TOPK - 0.5, s2[:, :], ALU.is_ge, ALU.max))
            link(dve.tensor_tensor(g2[:, :, :], expd[:, :, :], per_tile(s4), ALU.is_equal))
            dve.tensor_scalar(s5[:, :], s3[:, :], TOPK - 0.5, None, ALU.is_lt)
            dve.tensor_reduce(s1[:, :], expd[:, :, :], AX, ALU.add)
            dve.wait_ge(const_ready, 2)
            link(dve.tensor_tensor_scan(g3[:, :, :].rearrange("p t e -> p (t e)"), expert_run[:, :],
                                        g2[:, :, :].rearrange("p t e -> p (t e)"), 0.0, ALU.mult, ALU.add))
            dve.reciprocal(s2[:, :], s1[:, :])
            dve.tensor_tensor(g1[:, :, :], expd[:, :, :], per_tile(s4), ALU.is_gt)
            link(dve.tensor_tensor(g3[:, :, :], g3[:, :, :], per_tile(s5), ALU.add))
            dve.tensor_tensor(prob[:, :, :], expd[:, :, :], per_tile(s2), ALU.mult)
            link(dve.scalar_tensor_tensor(g4[:, :, :], g3[:, :, :], float(TOPK), g2[:, :, :], ALU.is_le, ALU.mult))
            link(dve.tensor_tensor(g4[:, :, :], g4[:, :, :], g1[:, :, :], ALU.add))
            link(dve.tensor_tensor(g3[:, :, :], g4[:, :, :], prob[:, :, :], ALU.mult))

            bits = g3[:, :, :].rearrange("p t e -> p (t e)").bitcast(U16).rearrange("p (t e h) -> p t e h", e=E, h=2)
            link(dve.tensor_copy(upper[:, :, :], bits[:, :, :, 1]))
            for r, (half, shift, d) in enumerate(ROUNDS):
                n = 2 ** d - 1
                found = best[:, r + half, 0, :]
                if (half, r) == (1, len(UPPER_DIGITS)):
                    upper_found = best[:, r, 0, :].unsqueeze(1).broadcast_to([P, NT, E])
                    dve.tensor_tensor(below_all[:, :, :], upper[:, :, :], upper_found, ALU.is_gt)
                    link(dve.tensor_tensor(same_upper[:, :, :], upper[:, :, :], upper_found, ALU.is_equal))
                    dve.tensor_copy(thr_upper[:, :], best[:, r, 0, :])
                    link(dve.tensor_tensor(same_upper[:, :, :], same_upper[:, :, :], lower[:, :, :], ALU.mult))
                    dve.scalar_tensor_tensor(keys[:, :, :], below_all[:, :, :], float(2 ** 16 - 1), same_upper[:, :, :],
                                             ALU.mult, ALU.max)
                    dve.tensor_scalar(thr_upper[:, :], thr_upper[:, :], 16, None, ALU.logical_shift_left)
                link(dve.scalar_tensor_tensor(cand[:, r % 2, 0:n, :], digits[:, 0:n, :], float(2 ** shift),
                                              found.unsqueeze(1).broadcast_to([P, n, E]), ALU.mult, ALU.add))
                source = keys if half else upper
                for t0, t1 in zip(CUTS, CUTS[1:]):
                    dve.tensor_tensor(hits[:, r % 2, 0:n, t0:t1, :],
                                      source[:, t0:t1, :].unsqueeze(1).broadcast_to([P, n, t1 - t0, E]),
                                      cand[:, r % 2, 0:n, :].unsqueeze(2).broadcast_to([P, n, t1 - t0, E]),
                                      ALU.is_ge).then_inc(compared, 1)
                if r == 0:
                    dve.tensor_copy(lower[:, :, :], bits[:, :, :, 0])
                if r == 1:
                    dve.tensor_copy(rows[:, :, C:ROW], g3[:, :, :]).then_inc(routed_ready, 1)
                if r == 2:
                    dve.wait_ge(b1T_done, 1)
                    dve.tensor_copy(b1T[:, :], ps_T[:, 0:E * HC])
                dve.wait_ge(summed, r + 1)
                link(dve.scalar_tensor_tensor(best[:, r + half, 1:1 + n, :],
                                              ps_cnt[:, 0:n * E].rearrange("p (n e) -> p n e", e=E), CAP - 0.5,
                                              cand[:, r % 2, 0:n, :], ALU.is_ge, ALU.mult))
                link(dve.tensor_reduce(best[:, r + half + 1, 0, :], best[:, r + half, 0:1 + n, :].rearrange("p n e -> p e n"),
                                       AX, ALU.max))
            link(dve.tensor_copy(thr_lower[:, :], best[:, NR + 1, 0, :]))
            link(dve.tensor_tensor(thr[:, :], thr_lower[:, :], thr_upper[:, :], ALU.bitwise_or))

            weight = g3[:, :, :].rearrange("p t e -> p e t")
            threshold = thr[:, :].bitcast(F32).unsqueeze(2).broadcast_to([P, E, NT])
            dve.tensor_tensor(member[:, 0], weight, threshold, ALU.is_gt)
            link(dve.tensor_tensor(member[:, 1], weight, threshold, ALU.is_equal))
            dve.tensor_tensor_scan(members[:, :, :, :].rearrange("p k e t -> p (k e t)"),
                                   tile_run[:, :, :, :].rearrange("p k e t -> p (k e t)"),
                                   member[:, :, :, :].rearrange("p k e t -> p (k e t)"), 0.0,
                                   ALU.mult, ALU.add).then_inc(member_ready, 1)
            dve.wait_ge(run_done, 1)
            run = ps_run.rearrange("p (k e t) -> p k e t", k=2, e=E)
            places = need[:, :].unsqueeze(2).broadcast_to([P, E, NT])
            link(dve.tensor_scalar(need[:, :], ps_total, -1.0, float(CAP), ALU.mult, ALU.add))
            dve.tensor_tensor(fits[:, :, :], run[:, 1], places, ALU.is_le)
            link(dve.tensor_tensor(capped[:, :, :], run[:, 1], places, ALU.min))
            dve.tensor_tensor(fits[:, :, :], fits[:, :, :], member[:, 1], ALU.mult)
            link(dve.tensor_tensor(pos[:, :, :], capped[:, :, :], run[:, 0], ALU.add))
            link(dve.tensor_tensor(taken[:, :, :], fits[:, :, :], member[:, 0], ALU.add))
            link(dve.tensor_tensor(pos[:, :, :], pos[:, :, :], taken[:, :, :], ALU.mult))

            link(dve.tensor_scalar(slot[:, :], pos[:, :, :].rearrange("p e t -> p (e t)"), 1.0, None, ALU.subtract))
            dve.tensor_scalar(maj[:, :], slot[:, :], MAJ - 1, None, ALU.bitwise_and)
            link(dve.tensor_scalar(cm[:, :], slot[:, :], MAJ.bit_length() - 1, None, ALU.logical_shift_right))

            def col(a, e, n):
                return a[:, e * NT:(e + 1) * NT].unsqueeze(2).broadcast_to([P, NT, n])

            def onehot_cm(e):
                dve.tensor_tensor(oh_cm[:, e], col(cm, e, CM), iota_cm[:, :].unsqueeze(1).broadcast_to([P, NT, CM]),
                                  ALU.is_equal)

            def onehot_maj(e):
                link(dve.tensor_tensor(oh_maj[:, e], col(maj, e, MAJ),
                                       iota_maj[:, :].unsqueeze(1).broadcast_to([P, NT, MAJ]), ALU.is_equal))

            def onehot_tok(e):
                dve.tensor_tensor(oh_tok[:, e], oh_maj[:, e], token_id[:, :].unsqueeze(2).broadcast_to([P, NT, MAJ]),
                                  ALU.mult).then_inc(onehot_ready, 1)

            def copy_grid(e):
                dve.wait_ge(grid_done, e + 1)
                dve.tensor_copy(grid[:, e, :], ps_grid[0:MAJ, 0:CM]).then_inc(grid_ready, 1)

            def copy_index(e):
                dve.wait_ge(index_done, e + 1)
                n = NC + e % 2
                dve.tensor_copy(index[:, e, 0:n], ps_grid[:, 64:64 + n]).then_inc(index_ready, 1)

            def tokens_in(e):
                dve.wait_ge(xgT_done, e + 1)
                if e >= 2:
                    dve.wait_ge(h_done, HC * (e - 1))
                dve.tensor_copy(xgT[:, e % 2, :], ps_x[:, 0:CAP]).then_inc(xgT_ready, 1)

            def weigh_bias(e):
                at, last = e % 2 * HALF, CHUNKS[LAST][1]
                tail = slice(at, at + last)
                mine = slice(e % 2 * LAST, (e % 2 + 1) * LAST)
                dve.wait_ge(xgT_done, e + 1)
                if e >= 2:
                    dve.wait_ge(y_ready, NC * (e - 1))
                dve.tensor_tensor(wb2[:, e % 2, 0:LAST, :], b2_sb[:, e, :].unsqueeze(1).broadcast_to([P, LAST, C]),
                                  xg[:, e // 2, mine, C + e:C + e + 1].broadcast_to([P, LAST, C]), ALU.mult)
                link(dve.tensor_scalar(wb2[tail, e % 2, LAST, :], b2_sb[tail, e, :], xg[tail, e // 2, 2 * LAST, C + e:C + e + 1],
                                       None, ALU.mult))

            def tokens_out(e):
                for c, (_, n) in enumerate(CHUNKS):
                    at = e % 2 * HALF if c == LAST else 0
                    own = slice(at, at + n)
                    dve.wait_ge(y_done, NC * e + c + 1)
                    dve.scalar_tensor_tensor(y[0:n, e, c, :], ps_ys[(NC * e + c) % 2][own, 0:C],
                                             xg_chunk(e, c)[:, C + e:C + e + 1], wb2[own, e % 2, c, :],
                                             ALU.mult, ALU.add).then_inc(y_ready, 1)

            onehot_cm(0)
            onehot_maj(0)
            onehot_tok(0)
            for e in range(E - 2):
                onehot_cm(e + 1)
                onehot_maj(e + 1)
                copy_grid(e)
                onehot_tok(e + 1)
                copy_index(e)
            dve.wait_ge(b_in, 32)
            weigh_bias(0)
            tokens_out(0)
            copy_grid(E - 2)
            onehot_cm(E - 1)
            onehot_maj(E - 1)
            onehot_tok(E - 1)
            copy_index(E - 2)
            weigh_bias(1)
            for e in range(1, E):
                if e + 1 < E:
                    tokens_in(e + 1)
                tokens_out(e)
                if e == 1:
                    copy_grid(E - 1)
                if e + 1 < E:
                    weigh_bias(e + 1)
                if e == 1:
                    copy_index(E - 1)

        @block.tensor
        def _(pe):

            def keep_warm(bank, times, width=512):
                for _ in range(times):
                    pe.matmul(bank[:, 0:width], warm_rhs[:, 0:P], warm_rhs[:, 0:width], start=True, stop=True)

            def transpose_x(b):
                pe.wait_ge(x_in[part_of(b)], 16)
                if b == 0:
                    pe.wait_ge(ident_ready, 1)
                else:
                    pe.wait_ge(T_copied, b)
                for i in range(TPB):
                    ins = pe.transpose(ps_T[:, i * P:(i + 1) * P], x_sb[:, b * TPB + i, :], ident[:, :])
                ins.then_inc(T_done, 1)

            def project(b):
                pe.wait_ge(T_copied, b + 1)
                if b == 0:
                    pe.wait_ge(wc_ready, 1)
                else:
                    pe.wait_ge(q_copied, 2 * b)
                pe.matmul(ps_q[:, 0:N], w_c[:, 0:C], xT[:, cols(b)], start=True, stop=True).then_inc(q_done, 1)
                if b >= 1:
                    pe.wait_ge(kv_copied, 4 * b)
                for i in range(TPB):
                    t = b * TPB + i
                    ins = pe.matmul(ps_kv[:, i * 2 * C:(i + 1) * 2 * C], xT[:, t * P:(t + 1) * P],
                                    w_c[:, C:3 * C], start=True, stop=True)
                ins.then_inc(kv_done, 1)

            def sum_q(b):
                pe.wait_ge(q_copied, 2 * b + 1)
                if b == 0:
                    pe.wait_ge(const_ready, 1)
                else:
                    pe.wait_ge(kqvar_ready, b)
                for i in range(TPB):
                    t = b * TPB + i
                    ins = pe.matmul(ps_qss[:, i * HEADS:(i + 1) * HEADS], qsqT[:, t * P:(t + 1) * P],
                                    head_mask[:, ::DH], start=True, stop=True)
                ins.then_inc(qss_done, 1)

            def correlate(b):
                if b == 0:
                    pe.wait_ge(vec_ready, 1)
                pe.wait_ge(kn_ready, b + 1)
                pe.wait_ge(kv_copied, 4 * (b + 1))
                if b >= 1:
                    pe.wait_ge(dots_ready, b)
                for i in range(TPB):
                    t = b * TPB + i
                    pe.matmul(ps_d[:, 0:P], kbeta_rows[:, :, :].rearrange("p h d -> p (h d)"), kv[:, t, C:2 * C], start=(i == 0), stop=False)
                for i in range(TPB):
                    t = b * TPB + i
                    ins = pe.matmul(ps_d[:, 0:P], kn[:, t, :], kv[:, t, C:2 * C], start=False, stop=(i == TPB - 1))
                ins.then_inc(d_done, 1)

            def attend(b):
                pe.wait_ge(q_copied, 2 * (b + 1))
                pe.wait_ge(dots_ready, b + 1)
                if b >= 1:
                    pe.wait_ge(o_used, b)
                for i in range(TPB):
                    t = b * TPB + i
                    pe.matmul(ps_o[:, i * P:(i + 1) * P], qT[:, t * P:(t + 1) * P], dots[:, b, :],
                              start=True, stop=True)
                pe.matmul(ps_o[:, TPB * P:TPB * P + P], q_cols[:, 1:2].broadcast_to([P, P]), dots[:, b, :],
                          start=True, stop=True).then_inc(o_done, 1)

            def transpose_x1(b):
                pe.wait_ge(x1_ready, b + 1)
                if b >= 1:
                    pe.wait_ge(T1_copied, b)
                for i in range(TPB):
                    ins = pe.transpose(ps_T1[:, i * P:(i + 1) * P], x1[:, b * TPB + i, :], ident[:, :])
                ins.then_inc(T1_done, 1)

            def gate(b):
                pe.wait_ge(T1_copied, b + 1)
                for i in range(TPB):
                    t = b * TPB + i
                    ins = pe.matmul(ps_logit[:, t * E:(t + 1) * E], x1T[:, t * P:(t + 1) * P], gateT[:, :],
                                    start=True, stop=True)
                ins.then_inc(logit_done, 1)

            pe.wait_ge(warm_ready, 1)
            keep_warm(ps_d, 4)
            transpose_x(0)
            keep_warm(ps_d, 3)
            pe.wait_ge(wv_ready, 1)
            pe.wait_ge(wh_ready, 1)
            pe.wait_ge(const_ready, 1)
            pe.matmul(ps_T1[:, 0:3 * C], col_mean[:, :], w_h[:, :], start=True, stop=True).then_inc(wmean_done, 1)
            transpose_x(1)
            pe.wait_ge(rows_ready, 1)
            for k in range(2):
                ins = pe.transpose(ps_small[:, k:k + 1], q_rows[0:1, k, :, :].rearrange("p h d -> p (h d)"), ident[0:1, 0:1])
            ins.then_inc(cols_T, 1)
            keep_warm(ps_d, 2)
            for s in range(STEPS):
                if s >= 1 and live(s + 1):
                    transpose_x(s + 1)
                if live(s - 1):
                    sum_q(s - 1)
                if live(s):
                    project(s)
                if live(s - 3):
                    attend(s - 3)
                if live(s - 2):
                    correlate(s - 2)
                if s == 2:
                    pe.wait_ge(gatec_ready, 1)
                    pe.wait_ge(cols_ready, 1)
                    pe.transpose(ps_small[:, 8:8 + E], gate_c[:, :], ident[0:E, 0:E]).then_inc(gate_T, 1)
                if live(s - 4):
                    transpose_x1(s - 4)
                if live(s - 5):
                    gate(s - 5)

            pe.wait_ge(b_in, 32)
            pe.transpose(ps_T[:, 0:E * HC], b1_rows[:, :], ident[0:E * HC, 0:E * HC]).then_inc(b1T_done, 1)
            keep_warm(ps_kv, 20)
            pe.wait_ge(const_ready, 2)
            for r, (_, _, d) in enumerate(ROUNDS):
                n = 2 ** d - 1
                for part, (t0, t1) in enumerate(zip(CUTS, CUTS[1:])):
                    pe.wait_ge(compared, (len(CUTS) - 1) * r + part + 1)
                    for t in range(t0, t1):
                        ins = pe.matmul(ps_cnt[:, 0:n * E], ones16[:, :], hits[:, r % 2, 0:n, t, :],
                                        start=(t == 0), stop=(t == NT - 1))
                ins.then_inc(summed, 1)
                keep_warm(ps_kv, 6, 2 * P)
            pe.wait_ge(member_ready, 1)
            pe.matmul(ps_run, upto[:, :], member[:, :, :, :].rearrange("p k e t -> p (k e t)"), start=True, stop=False)
            pe.matmul(ps_run, ones16[:, :], members[:, :, :, :].rearrange("p k e t -> p (k e t)"), start=False, stop=True)
            pe.matmul(ps_total, ones16[:, :], members[:, 0, :, NT - 1], start=True, stop=True).then_inc(run_done, 1)
            keep_warm(ps_kv, 4, 2 * P)

            def find_tokens(e):
                pe.wait_ge(onehot_ready, e + 1)
                if e >= 1:
                    pe.wait_ge(index_ready, e)
                for t in range(NT):
                    ins = pe.matmul(ps_grid[0:MAJ, 0:CM], oh_tok[:, e, t, :], oh_cm[:, e, t, :],
                                    start=(t == 0), stop=(t == NT - 1))
                ins.then_inc(grid_done, 1)

            def spread_tokens(e):
                pe.wait_ge(grid_ready, e + 1)
                by_chunk = grid[:, e, :].rearrange("a (c b) -> a c b", b=SUB)
                for b in range(SUB):
                    ins = pe.matmul(ps_grid[:, 64:64 + NC], spread[:, b, :], by_chunk[:, :, b],
                                    start=(b == 0), stop=(b == SUB - 1))
                half = slice(e % 2 * HALF, (e % 2 + 1) * HALF)
                for b in range(SUB // 2):
                    ins = pe.matmul(ps_grid[half, 64 + NC:64 + NC + 1], spread[:, b, 0:HALF], by_chunk[:, LAST:NC, b],
                                    start=(b == 0), stop=(b == SUB // 2 - 1))
                ins.then_inc(index_done, 1)

            def tokens_in(e):
                pe.wait_ge(gathered[e], 16 * LAST)
                pe.wait_ge(pair_gathered[e // 2], 16)
                if e >= 1:
                    pe.wait_ge(xgT_ready, e)
                for c, (at, n) in enumerate(CHUNKS):
                    rows_at = e % 2 * HALF if c == LAST else 0
                    own = slice(rows_at, rows_at + n)
                    ins = pe.transpose(ps_x[:, at:at + n], xg_chunk(e, c)[:, 0:C], ident[own, own])
                ins.then_inc(xgT_done, 1)

            def up_chunk(e, c):
                if e >= 1:
                    pe.wait_ge(h_ready, HC * (e - 1) + c + 1)
                pe.matmul(ps_h[c][:, 0:CAP], w1_sb[:, e, c * P:(c + 1) * P], xgT[:, e % 2, :],
                          start=True, stop=True).then_inc(h_done, 1)

            def up(e):
                pe.wait_ge(xgT_ready, e + 1)
                for c in range(HC):
                    up_chunk(e, c)

            def down_chunk(e, k):
                if NC * e + k >= 2:
                    pe.wait_ge(y_ready, NC * e + k - 1)
                at, n = CHUNKS[k]
                y_at = e % 2 * HALF if k == LAST else 0
                for c in range(HC):
                    if k == 0:
                        pe.wait_ge(h_ready, HC * e + c + 1)
                    ins = pe.matmul(ps_ys[(NC * e + k) % 2][y_at:y_at + n, 0:C], hid[:, e % 2, c, at:at + n],
                                    w2_sb[:, e, c, :], start=(c == 0), stop=(c == HC - 1))
                ins.then_inc(y_done, 1)

            def down(e):
                for k in range(NC):
                    down_chunk(e, k)

            def look_up(e0, e1):
                for e in range(e0, e1):
                    find_tokens(e)
                    keep_warm(ps_kv, 2)
                    spread_tokens(e)
                    keep_warm(ps_kv, 2)

            early = E // 2
            look_up(0, early)
            tokens_in(0)
            pe.wait_ge(w1_in, 16)
            pe.wait_ge(w2_in, 16)
            pe.wait_ge(xgT_ready, 1)
            up_chunk(0, 0)
            up_chunk(0, 1)
            find_tokens(early)
            up_chunk(0, 2)
            spread_tokens(early)
            up_chunk(0, 3)
            find_tokens(early + 1)
            tokens_in(1)
            spread_tokens(early + 1)
            down(0)
            find_tokens(early + 2)
            pe.wait_ge(xgT_ready, 2)
            up_chunk(1, 0)
            up_chunk(1, 1)
            spread_tokens(early + 2)
            up_chunk(1, 2)
            up_chunk(1, 3)
            tokens_in(2)
            down(1)
            find_tokens(early + 3)
            pe.wait_ge(xgT_ready, 3)
            up_chunk(2, 0)
            up_chunk(2, 1)
            spread_tokens(early + 3)
            up_chunk(2, 2)
            up_chunk(2, 3)
            tokens_in(3)
            down(2)
            for e in range(3, E):
                up(e)
                if e + 1 < E:
                    tokens_in(e + 1)
                down(e)


_INS = ['x', 'L0_conv_w_qkv', 'L0_conv_q_gamma', 'L0_conv_q_beta', 'L0_conv_k_gamma', 'L0_conv_k_beta',
        'L0_ffn_gate_w', 'L0_ffn_gate_b', 'L0_ffn_w1', 'L0_ffn_b1', 'L0_ffn_w2', 'L0_ffn_b2']


def kernel(**inputs):
    import numpy as _np
    import concourse.bacc as _bacc
    from concourse import mybir as _mybir
    from concourse.bass_utils import run_bass_kernel_spmd as _run

    nc = _bacc.Bacc("TRN2", target_bir_lowering=False, num_devices=1)
    arrays, args = {}, []
    for name in _INS:
        a = _np.ascontiguousarray(inputs[name])
        arrays[f"in_{name}_dram"] = a
        args.append(nc.dram_tensor(f"in_{name}_dram", a.shape, _mybir.dt.from_np(a.dtype), kind="ExternalInput").ap())
    shape = inputs['x'].shape
    out = nc.dram_tensor("out_0_dram", shape, _mybir.dt.float32, kind="ExternalOutput").ap()
    build(nc, *args, out)
    r = _run(nc, [arrays], core_ids=[0])
    return r.results[0]["out_0_dram"]
```
